# Optimizing a Trainium2 kernel written in Bass

```python
import numpy as np
import jax
import jax.numpy as jnp

def _softmax(x, axis=-1):
    return jax.nn.softmax(x, axis=axis)

def _gelu(x):
    return jax.nn.gelu(x, approximate=True)

def _silu(x):
    return jax.nn.silu(x)

def _sigmoid(x):
    return jax.nn.sigmoid(x)

def _layernorm(x, axis=-1, eps=1e-05):
    m = jnp.mean(x, axis=axis, keepdims=True)
    v = jnp.var(x, axis=axis, keepdims=True)
    return (x - m) / jnp.sqrt(v + eps)

def _scatter_add(tgt, idx, src, axis=0):
    return tgt.at[idx].add(src)

def _segment_sum(src, seg, n):
    return jax.ops.segment_sum(src, seg, n)
kernel_name = 'mk_gnn_preln_d1_gnn_r32_5e6e5a'

def setup_inputs(seed: int=0):
    np.random.seed(seed)
    _w = jnp.asarray

    def _rec_inputs():
        import jax
        import jax.numpy as jnp
        _gk = jax.random.key(seed)
        x = -0.0003713 + 1 * jax.random.normal(jax.random.fold_in(_gk, 1), (50000, 256), jnp.float32)
        src = jax.random.randint(jax.random.fold_in(_gk, 2), (25000,), 0, 50000, jnp.int32)
        dst = jnp.minimum((50000 * jax.random.uniform(jax.random.fold_in(_gk, 3), (25000,)) ** 2.0).astype(jnp.int32), 49999)
        _o = jnp.argsort(dst, stable=True)
        src = src[_o]
        dst = dst[_o]
        edge_attr_256 = -6.47781e-05 + 0.999943 * jax.random.normal(jax.random.fold_in(_gk, 12), (25000, 256), jnp.float32)
        return (x, src, dst, edge_attr_256)
    x, src, dst, edge_attr_256 = _rec_inputs()

    def _L0_gnn_setup():
        import jax, jax.numpy as jnp
        import numpy as np
        N_NODES = 50000
        N_EDGES = 25000
        DIM2 = 256
        N_TYPES = 256
        N_HEADS = 4
        TEMP = 1.0
        key = jax.random.key(seed)
        ks = jax.random.split(key, 8)
        src_embedding = jax.random.normal(ks[0], (N_NODES, DIM2), jnp.float32)
        edge_embedding = jax.random.normal(ks[1], (N_EDGES, DIM2), jnp.float32)
        src_idx = jax.random.randint(ks[2], (N_EDGES,), 0, N_NODES)
        dst_idx = jax.random.randint(ks[3], (N_EDGES,), 0, N_NODES)
        W_fc = jax.random.normal(ks[4], (N_TYPES, DIM2), jnp.float32) / np.sqrt(DIM2)
        b_fc = jnp.zeros((N_TYPES,), jnp.float32)
        Q = jax.random.normal(ks[5], (N_HEADS, N_TYPES), jnp.float32) / np.sqrt(N_TYPES)
        Wg = jax.random.normal(ks[6], (N_HEADS, N_TYPES), jnp.float32) / np.sqrt(N_TYPES)
        bg = jnp.zeros((N_HEADS,), jnp.float32)
        return {'src_embedding': src_embedding, 'edge_embedding': edge_embedding, 'W_fc': W_fc, 'b_fc': b_fc, 'Q': Q, 'Wg': Wg, 'bg': bg, 'src_idx': src_idx, 'dst_idx': dst_idx}
    _L0_gnn_all = _L0_gnn_setup()
    _L0_gnn_in = {k: v for k, v in _L0_gnn_all.items() if k in ('W_fc', 'b_fc', 'Q', 'Wg', 'bg')}
    del _L0_gnn_all
    return {'x': x, 'src': src, 'dst': dst, 'edge_attr_256': edge_attr_256, 'L0_gnn_W_fc': _L0_gnn_in['W_fc'], 'L0_gnn_b_fc': _L0_gnn_in['b_fc'], 'L0_gnn_Q': _L0_gnn_in['Q'], 'L0_gnn_Wg': _L0_gnn_in['Wg'], 'L0_gnn_bg': _L0_gnn_in['bg']}

def reference(x, src, dst, edge_attr_256, L0_gnn_W_fc, L0_gnn_b_fc, L0_gnn_Q, L0_gnn_Wg, L0_gnn_bg):
    import jax
    import jax.numpy as jnp

    def _L0_gnn_ref(src_embedding, edge_embedding, W_fc, b_fc, Q, Wg, bg, src_idx, dst_idx):
        import jax, jax.numpy as jnp
        import numpy as np
        N_NODES = 50000
        N_EDGES = 25000
        DIM2 = 256
        N_TYPES = 256
        N_HEADS = 4
        TEMP = 1.0
        msg = jax.nn.relu(src_embedding[src_idx] + edge_embedding)
        p = msg @ W_fc.T + b_fc
        scores = p @ Q.T / TEMP
        smax = jax.ops.segment_max(scores, dst_idx, num_segments=N_NODES)
        smax = jnp.where(jnp.isfinite(smax), smax, 0.0)
        w = jnp.exp(scores - smax[dst_idx])
        denom = jax.ops.segment_sum(w, dst_idx, num_segments=N_NODES)
        alpha = w / jnp.maximum(denom[dst_idx], 1e-09)
        pooled = jnp.stack([jax.ops.segment_sum(alpha[:, h:h + 1] * p, dst_idx, num_segments=N_NODES) for h in range(N_HEADS)], axis=1)
        deg = jax.ops.segment_sum(jnp.ones((p.shape[0],), p.dtype), dst_idx, num_segments=N_NODES)
        mean_p = jax.ops.segment_sum(p, dst_idx, num_segments=N_NODES) / jnp.maximum(deg, 1.0)[:, None]
        gate = jax.nn.softmax(mean_p @ Wg.T + bg, axis=-1)
        predict = jax.nn.sigmoid(jnp.einsum('nh,nht->nt', gate, pooled))
        return predict
    h = jnp.maximum(_layernorm(x, axis=-1), 0.0)
    x = x + _L0_gnn_ref(h, edge_attr_256, L0_gnn_W_fc, L0_gnn_b_fc, L0_gnn_Q, L0_gnn_Wg, L0_gnn_bg, src, dst)
    return x

_drawn_inputs = setup_inputs


def setup_inputs(seed=0):
    import zlib

    import numpy as np

    out = dict(_drawn_inputs(seed))
    spreads = {'L0_gnn_b_fc': (0.0, 0.737), 'L0_gnn_bg': (0.0, 0.8)}
    factors = {'L0_gnn_Q': 6.237, 'L0_gnn_Wg': 8.0}
    for name, (base, spread) in spreads.items():
        noise = np.random.default_rng([zlib.crc32(name.encode()), seed]).standard_normal(out[name].shape)
        drawn = base * np.exp(spread * noise) if base else spread * noise
        out[name] = jnp.asarray(drawn.astype(out[name].dtype))
    for name, factor in factors.items():
        out[name] = (out[name] * factor).astype(out[name].dtype)
    return out
```

```python
from contextlib import ExitStack

import concourse.bass as bass
from concourse import mybir

F32 = mybir.dt.float32
I32 = mybir.dt.int32
ALU = mybir.AluOpType
ACT = mybir.ActivationFunctionType
AX = mybir.AxisListType

P = 128
BIG = 1.0e30
LN_EPS = 1e-5
BODY = 16
LEAD = 6
LAG = 4
UNROLL = 16


def gnn_layer(nc, x, src, dst, edge_attr, w_fc, b_fc, q_w, g_w, b_g, out):
    N, D = x.shape
    E = src.shape[0]
    T = w_fc.shape[0]
    H = q_w.shape[0]
    K = 2 * H
    C = 2 * H + 1
    KD, KT = D // P, T // P
    TILES = -(-E // P)
    LAST = E - (TILES - 1) * P
    BLK = -(-TILES // P)
    TP = BLK * P
    NODES = -(-N // P)
    STEPS = TILES + NODES
    PAD = 1 << 16
    SHIFT = P.bit_length() - 1
    NT = T + K
    FOURS = STEPS // 4
    SPREADS = 8
    assert (FOURS - 2) % 8 == 0
    assert BLK == 2 and KD == 2 and KT == 2 and N < PAD and H == 4

    BODIES = TILES // BODY
    SPLIT = 8
    RING = SPLIT * BODY - LAG
    STAGE = 8
    SPILL = TILES - RING
    assert RING % 4 == 0 and SPILL % 4 == 0 and SPILL <= RING and (RING + LAG) % BODY == 0

    GROUP = 4
    GROUPS = -(-NODES // GROUP)
    FULL = N // (GROUP * P)
    assert GROUPS == FULL + 1 and FULL % 2 == 1
    LAST_WHOLE = (N - FULL * GROUP * P) // P
    LOOPED = (FULL - 3) // 4 * 4
    XS, YS = 4, 4
    assert FULL % 4 == 1 and LAST_WHOLE == 2 and N % P and LOOPED + 3 < FULL

    scratch = nc.dram_tensor("p_spill", [SPILL * P, T], F32).ap()

    with ExitStack() as ctx:
        def sb(name, shape, dt=F32):
            return ctx.enter_context(nc.sbuf_tensor(name, shape, dt))

        def sem(name):
            return ctx.enter_context(nc.semaphore(name))

        bank = ctx.enter_context(nc.psum_tensor("bank", [P, 8, 512], F32))

        p_keep = sb("p_keep", [P, RING + STAGE, T])
        arena = sb("arena", [P, 10240])
        logits = sb("logits", [P, TP, K])
        w_all = sb("w_all", [P, KD, NT])
        bias = sb("bias", [P, NT])
        ident = sb("ident", [P, P])
        ones = sb("ones", [P, P])
        zeros = sb("zeros", [P, T], mybir.dt.bfloat16)
        step_f = sb("step_f", [P, STEPS])
        sel = sb("sel", [P, BLK, STEPS])
        rel = sb("rel", [P, STEPS])
        wgt = sb("wgt", [P, STEPS])
        dst_f = sb("dst_f", [P, BLK, P])
        idx = sb("idx", [P, TP], I32)
        idx_slot = sb("idx_slot", [P, BODY], I32)
        spread = sb("spread", [P, SPREADS, P])
        stats = sb("stats", [P, BODY, 6])
        mv = sb("mv", [P, BODY, 2])
        rstd = sb("rstd", [P, BODY])
        negmr = sb("negmr", [P, BODY])
        eps = sb("eps", [P, 1])
        bg_b = sb("bg_b", [P, H])
        tile_f = sb("tile_f", [P, BLK])
        tile_i = sb("tile_i", [P, BLK], I32)
        s_done = sb("s_done", [P, BLK])
        node_of = sb("node_of", [P, BLK])
        node_i = sb("node_i", [P, BLK], I32)
        by_s = sb("by_s", [P, STEPS], I32)
        walk_bank, walk_p = by_s[0:1, :], by_s[32:33, :]
        by_n = sb("by_n", [P, NODES + 1], I32)
        tile_end, need_p, need_bank, node_end = (by_n[32 * n:32 * n + 1, :] for n in range(4))

        o = 0
        xg = arena[:, o:o + BODY * D].rearrange("p (t d) -> p t d", d=D); o += BODY * D
        ea = arena[:, o:o + BODY * D].rearrange("p (t d) -> p t d", d=D); o += BODY * D
        u = arena[:, o:o + 4 * D].rearrange("p (t d) -> p t d", d=D); o += 4 * D
        msg_t = arena[:, o:o + 4 * D].rearrange("p (t c e) -> p t c e", c=KD, e=P); o += 4 * D
        assert o <= 10240
        o = 0
        RW = BLK * P
        val = arena[:, o:o + C * RW].rearrange("p (k e) -> p k e", k=C); o += C * RW
        run = arena[:, o:o + C * RW].rearrange("p (k e) -> p k e", k=C); o += C * RW
        tot = arena[:, o:o + C * RW].rearrange("p (k e) -> p k e", k=C); o += C * RW
        flag = arena[:, o:o + 6 * RW].rearrange("p (k e) -> p k e", k=6); o += 6 * RW
        row_b = arena[0:C, o:o + 6 * (TP + 1)].rearrange("p (k t) -> p k t", k=6); o += 6 * (TP + 1)
        carry = arena[:, o:o + BLK * 2 * C].rearrange("p (b s k) -> p b s k", b=BLK, s=2); o += BLK * 2 * C
        assert o <= 10240
        row_a = logits[0:C, :, :].rearrange("p t k -> p (t k)")[:, 0:7 * (TP + 1)].rearrange("p (k t) -> p k t", k=7)
        ends = tot[:, 0, 0:BLK * 2 * C].rearrange("p (b s k) -> p b s k", b=BLK, s=2)
        xin = arena[:, 0:XS * GROUP * D].rearrange("p (s q d) -> p s q d", s=XS, q=GROUP)
        yout = arena[:, XS * GROUP * D:(XS + YS) * GROUP * D].rearrange("p (s q d) -> p s q d", s=YS, q=GROUP)
        tail = p_keep[:, RING - 20:RING, :].rearrange("p t d -> p (t d)")
        o = 0
        w_nat = tail[:, o:o + KT * D].rearrange("p (c d) -> p c d", c=KT); o += KT * D
        b_rep = tail[:, o:o + KT * P].rearrange("p (c e) -> p c e", c=KT); o += KT * P
        q_t = tail[:, o:o + KT * K].rearrange("p (c k) -> p c k", c=KT); o += KT * K
        qg = tail[0:K, o:o + T]; o += T
        b_col = tail[:, o:o + KT]; o += KT
        done = tail[:, o:o + BLK * STEPS].rearrange("p (b s) -> p b s", b=BLK); o += BLK * STEPS
        i_of = tail[:, o:o + STEPS]; o += STEPS
        j_of = tail[:, o:o + STEPS + 1]; o += STEPS + 1
        step_i = tail[:, o:o + STEPS].bitcast(I32); o += STEPS
        rel_tmp = tail[:, o:o + STEPS]; o += STEPS
        src_f = tail[:, o:o + TP].rearrange("p (b e) -> p b e", b=BLK); o += TP
        assert o <= 20 * T
        src_i = p_keep[:, RING - 22, :].rearrange("p (b e) -> p b e", b=BLK).bitcast(I32)
        dst_i = p_keep[:, RING - 21, :].rearrange("p (b e) -> p b e", b=BLK).bitcast(I32)

        pads_set = sem("pads_set")
        src_in, dst_in, w_in = sem("src_in"), sem("dst_in"), sem("w_in")
        const_set = sem("const_set")
        src_f32, src_turned, idx_ready = sem("src_f32"), sem("src_turned"), sem("idx_ready")
        w_turned, qg_turned, q_t_ready, b_ready = sem("w_turned"), sem("qg_turned"), sem("q_t_ready"), sem("b_ready")
        wq_done, w_ready = sem("wq_done"), sem("w_ready")
        done_ready, i_summed, sel_ready = sem("done_ready"), sem("i_summed"), sem("sel_ready")
        rel_summed, ended_ready, end_summed = sem("rel_summed"), sem("ended_ready"), sem("end_summed")
        tables_ready = sem("tables_ready")
        dve_step, pool_step = sem("dve_step"), sem("pool_step")
        idx_copied, idx_seen, stats_seen = sem("idx_copied"), sem("idx_seen"), sem("stats_seen")
        gathered = [sem(f"gathered{k}") for k in range(BODY)]
        ea_in = [sem(f"ea_in{k}") for k in range(4)]
        stats_done, mv_done = sem("stats_done"), sem("mv_done")
        std_done, rstd_done, norm_ready = sem("std_done"), sem("rstd_done"), sem("norm_ready")
        ln_done, added, turned, relu_done = sem("ln_done"), sem("added"), sem("turned"), sem("relu_done")
        multiplied, p_out, padded = sem("multiplied"), sem("p_out"), sem("padded")
        spilled = [sem("spilled0"), sem("spilled1")]
        rows_turned, ends_turned, carries_ready = sem("rows_turned"), sem("ends_turned"), sem("carries_ready")
        totals_ready, carries_turned = sem("totals_ready"), sem("carries_turned")
        diff_ready, exp_done = sem("diff_ready"), sem("exp_done")
        c_ready, wgt_summed, wgt_ready = sem("c_ready"), sem("wgt_summed"), sem("wgt_ready")
        spread_ready, stepped = sem("spread_ready"), sem("stepped")
        p_ready, reloaded = sem("p_ready"), sem("reloaded")
        sig_done, bank_zero, summed = sem("sig_done"), sem("bank_zero"), sem("summed")
        x_in = [sem(f"x_in{k}") for k in range(XS)]
        stored = [sem(f"stored{k}") for k in range(YS)]

        t0_late = [False]

        def stage1(eng, tick):
            for k in range(-LEAD, BODY):
                tick(0, k, True)
            for a, b in ((1, SPLIT), (SPLIT, BODIES - 1)):
                t0_late[0] = a == SPLIT
                with eng.Fori(a, b) as body:
                    t0 = body * BODY
                    for k in range(BODY):
                        tick(t0, k, False)
            for k in range((BODIES - 1) * BODY, TILES + LAG):
                tick(0, k, True)

        block = ctx.enter_context(nc.Block())

        @block.sync
        def _(sp):
            sp.wait_ge(pads_set, 2)
            for half in range(2):
                sp.sem_inc(spilled[half], 16)
            for dram, tile, done_ in ((src, src_i, src_in), (dst, dst_i, dst_in)):
                whole = (TILES - 1) * P
                sp.dma_start(tile[:, 0, :], dram[0:P * P].rearrange("(t e) -> t e", e=P)).then_inc(done_, 16)
                sp.dma_start(tile[0:TILES - 1 - P, 1, :],
                             dram[P * P:whole].rearrange("(t e) -> t e", e=P)).then_inc(done_, 16)
                sp.dma_start(tile[TILES - 1 - P:TILES - P, 1, 0:LAST],
                             dram[whole:E].rearrange("(t e) -> t e", t=1)).then_inc(done_, 16)
            sp.dma_start(w_nat, w_fc.rearrange("(c p) d -> p c d", p=P)).then_inc(w_in, 16)
            sp.dma_start(qg[0:H, :], q_w).then_inc(w_in, 16)
            sp.dma_start(qg[H:K, :], g_w).then_inc(w_in, 16)
            with nc.allow_non_contiguous_dma(reason="one column of biases, once"):
                sp.dma_start(b_col, b_fc.rearrange("(c p) -> p c", p=P)).then_inc(w_in, 16)
            sp.dma_start(bias[:, 0:T], b_fc.rearrange("(a n) -> a n", a=1).broadcast_to([P, T])).then_inc(w_in, 16)
            sp.dma_start(bg_b[:, :], b_g.rearrange("(a n) -> a n", a=1).broadcast_to([P, H])).then_inc(w_in, 16)

            ea_rows = edge_attr[0:(TILES - 1) * P, :].rearrange("(t p) d -> p t d", p=P)

            def load_ea(t0, quad, first=False):
                if not first:
                    sp.wait_ge(added, t0 + 4 * quad - BODY + 4)
                sp.dma_start(ea[:, 4 * (quad % 4):4 * (quad % 4) + 4, :],
                             ea_rows[:, bass.ds(t0 + 4 * quad, 4), :]).then_inc(ea_in[quad % 4], 16)

            for quad in range(4):
                load_ea(0, quad, True)
            with sp.Fori(1, SPLIT) as body:
                t0 = body * BODY
                for quad in range(4):
                    load_ea(t0, quad)

            def spill(n4, half):
                sp.wait_ge(p_out, RING + n4 + 4)
                sp.dma_start(scratch[bass.ds(n4 * P, 4 * P), :].rearrange("(t p) d -> p t d", p=P),
                             p_keep[:, RING + 4 * half:RING + 4 * half + 4, :]).then_inc(spilled[half], 16)

            with sp.Fori(SPLIT, BODIES) as body:
                t0 = body * BODY
                for quad in range(4):
                    load_ea(t0, quad)
                    spill(t0 + 4 * quad - SPLIT * BODY, quad % 2)
            t0 = BODIES * BODY
            sp.wait_ge(added, t0 - BODY + 4)
            sp.dma_start(ea[:, 0:3, :], ea_rows[:, t0:t0 + 3, :]).then_inc(ea_in[0], 16)
            sp.dma_start(ea[0:LAST, 3, :], edge_attr[(TILES - 1) * P:E, :]).then_inc(ea_in[0], 16)
            n4 = t0 - SPLIT * BODY
            while n4 < SPILL:
                spill(n4, (n4 // 4) % 2)
                n4 += 4
            for half in range(2):
                sp.wait_ge(spilled[half], 16 + 16 * len(range(half, SPILL // 4, 2)))

            sp.wait_ge(tables_ready, 1)
            sp.wait_ge(c_ready, 1)
            sp.sem_inc(p_ready, RING)
            with sp.Fori(0, SPILL, 1) as n:
                end = sp.value_load(tile_end[0:1, bass.ds(n, 1)], min_val=1, max_val=STEPS)
                sp.wait_ge(stepped, end)
                sp.dma_start(p_keep[:, bass.ds(n, 1), :].rearrange("p t d -> p (t d)"),
                             scratch[bass.ds(n * P, P), :]).then_inc(reloaded, 16)
                sp.wait_ge(reloaded, 16 * n + 16)
                sp.sem_inc(p_ready, 1)

        @block.gpsimd
        def _(pool):
            pool.memset(src_i, 0).then_inc(pads_set, 1)
            pool.memset(dst_i, PAD).then_inc(pads_set, 1)
            pool.memset(ident[:, :], 0.0).then_inc(pool_step, 1)
            pool.wait_ge(pool_step, 1)
            pool.affine_select(out=ident[:, :], in_=ident[:, :], compare_op=ALU.not_equal, fill=1.0, base=0,
                               pattern=[[-1, P]], channel_multiplier=1).then_inc(const_set, 1)
            pool.memset(ones[:, :], 1.0).then_inc(const_set, 1)
            pool.memset(zeros[:, :], 0.0).then_inc(const_set, 1)
            pool.iota(step_i, pattern=[[1, STEPS]], base=0, channel_multiplier=0).then_inc(const_set, 1)
            pool.iota(tile_i[:, :], pattern=[[P, BLK]], base=0, channel_multiplier=1).then_inc(const_set, 1)
            pool.memset(eps[:, :], LN_EPS).then_inc(const_set, 1)
            pool.memset(logits[:, TILES - 1:TP, :], 0.0).then_inc(const_set, 1)
            pool.wait_ge(idx_ready, 1)

            def gather(t0, k, n=P, first=False):
                if not first:
                    pool.wait_ge(ln_done, t0 + k - BODY + 1)
                pool.tensor_copy(idx_slot[:, k:k + 1], idx[:, bass.ds(t0 + k, 1)]).then_inc(idx_copied, 1)
                pool.wait_ge(idx_copied, t0 + k + 1)
                pool.sem_inc(idx_seen, 1)
                pool.indirect_dma_start(out=xg[0:n, k, :], out_offset=None, in_=x,
                                        in_offset=bass.IndirectOffsetOnAxis(ap=idx_slot[0:n, k:k + 1], axis=0),
                                        ).then_inc(gathered[k], 16)

            for k in range(BODY):
                gather(0, k, first=True)
            with pool.Fori(1, BODIES) as body:
                t0 = body * BODY
                for k in range(BODY):
                    gather(t0, k)
            for k in range(TILES - BODIES * BODY):
                gather(BODIES * BODY, k, LAST if BODIES * BODY + k == TILES - 1 else P)

            with pool.Fori(0, FULL // 4) as four:
                g0 = four * 4
                for slot in range(4):
                    pool.wait_ge(sig_done, g0 + slot + 1)
                    pool.wait_ge(x_in[slot], g0 * 4 + 16)
                    pool.tensor_tensor(yout[:, slot, :, :], yout[:, slot, :, :], xin[:, slot, :, :],
                                       ALU.add).then_inc(summed, 1)
            for g in range(FULL - FULL % 4, GROUPS):
                slot = g % 4
                pool.wait_ge(sig_done, g + (2 if g == FULL else 1))
                pool.wait_ge(x_in[slot], 16 * (g // 4) + 16 + (16 if g == FULL else 0))
                whole = GROUP if g < FULL else (N - g * GROUP * P) // P
                ins = pool.tensor_tensor(yout[:, slot, 0:whole, :], yout[:, slot, 0:whole, :],
                                         xin[:, slot, 0:whole, :], ALU.add)
                if g == FULL:
                    left = N % P
                    ins.then_inc(pool_step, 1)
                    pool.wait_ge(pool_step, 2)
                    ins = pool.tensor_tensor(yout[0:left, slot, whole, :], yout[0:left, slot, whole, :],
                                             xin[0:left, slot, whole, :], ALU.add)
                ins.then_inc(summed, 1)

        @block.scalar
        def _(act):
            def tick(t0, k, edge):
                t = t0 + k
                m = k % BODY
                if not edge or 0 <= t < TILES:
                    act.wait_ge(norm_ready, (t0 // 4) + k // 4 + 1)
                    if not edge or t >= 4:
                        act.wait_ge(turned, t - 4 + 1)
                    n = LAST if edge and t == TILES - 1 else P
                    nc.scalar.activation(u[0:n, k % 4, :], xg[0:n, m, :], ACT.Relu, bias=negmr[0:n, m:m + 1],
                                         scale=rstd[0:n, m:m + 1]).then_inc(ln_done, 1)
                if not edge or 1 <= t <= TILES:
                    b = (k - 1) % 2
                    n = LAST if edge and t == TILES else P
                    act.wait_ge(turned, t)
                    if not edge or t >= 5:
                        act.wait_ge(multiplied, t - 4)
                    nc.scalar.activation(msg_t[:, (k - 1) % 4, :, 0:n],
                                         bank[:, b, 0:D].rearrange("p (c e) -> p c e", c=KD)[:, :, 0:n],
                                         ACT.Relu).then_inc(relu_done, 1)
                if k % 4 == (3 - LEAD + 1) % 4:
                    q = t + LEAD - 4
                    if not edge or 0 <= q < TILES:
                        m4 = (k + LEAD - 4) % BODY
                        n = P
                        act.wait_ge(mv_done, q + 4)
                        nc.scalar.activation(rstd[:, m4:m4 + 4], mv[:, m4:m4 + 4, 1], ACT.Sqrt,
                                             bias=eps[:, 0:1]).then_inc(std_done, 1)

            act.wait_ge(const_set, 7)
            stage1(act, tick)

            act.wait_ge(diff_ready, 1)
            nc.scalar.activation(val[:, 0:H, :], val[:, 0:H, :], ACT.Exp).then_inc(exp_done, 1)
            act.wait_ge(diff_ready, 2)
            nc.scalar.activation(run[:, H:K, :], run[:, H:K, :], ACT.Exp).then_inc(exp_done, 1)

            act.wait_ge(tables_ready, 1)
            act.wait_ge(wgt_ready, 1)
            act.sem_inc(bank_zero, 2)
            x_rows = x[0:FULL * GROUP * P, :].rearrange("(t p) d -> p t d", p=P)
            o_rows = out[0:FULL * GROUP * P, :].rearrange("(t p) d -> p t d", p=P)
            last_row = (FULL * GROUP + LAST_WHOLE) * P

            def load_x(g, slot):
                act.dma_start(xin[:, slot, :, :], x_rows[:, bass.ds(g * GROUP, GROUP), :]).then_inc(x_in[slot], 16)

            def load_last_x():
                slot = FULL % XS
                act.dma_start(xin[:, slot, 0:LAST_WHOLE, :],
                              x[FULL * GROUP * P:last_row, :].rearrange("(t p) d -> p t d", p=P)
                              ).then_inc(x_in[slot], 16)
                act.dma_start(xin[0:N % P, slot, LAST_WHOLE, :], x[last_row:N, :]).then_inc(x_in[slot], 16)

            def sigmoid(g, slot):
                end = act.value_load(node_end[0:1, bass.ds(g * GROUP + GROUP - 1, 1)], min_val=1, max_val=STEPS)
                act.wait_ge(stepped, end)
                b = GROUP * (slot % 2)
                nc.scalar.activation(yout[:, slot, :, :], bank[:, b:b + GROUP, 0:T], ACT.Sigmoid).then_inc(sig_done, 1)
                act.wait_ge(sig_done, g + 1)
                nc.scalar.activation(bank[:, b:b + GROUP, 0:T], zeros[:, :].unsqueeze(1).broadcast_to([P, GROUP, T]),
                                     ACT.Copy).then_inc(bank_zero, 1)

            def store(g, slot):
                act.wait_ge(summed, g + 1)
                act.dma_start(o_rows[:, bass.ds(g * GROUP, GROUP), :], yout[:, slot, :, :]).then_inc(stored[slot], 16)

            for g in range(3):
                load_x(g, g)
            for g in range(4):
                sigmoid(g, g)
                if g:
                    store(g - 1, g - 1)
                load_x(g + 3, (g + 3) % 4)
            with act.Fori(1, LOOPED // 4) as four:
                g0 = four * 4
                for slot in range(4):
                    act.wait_ge(stored[slot], 4 * g0)
                    sigmoid(g0 + slot, slot)
                    store(g0 + slot - 1, (slot - 1) % 4)
                    load_x(g0 + slot + 3, (slot + 3) % 4)
            for g in range(LOOPED, FULL):
                slot = g % 4
                act.wait_ge(stored[slot], 16 * (g // 4))
                sigmoid(g, slot)
                store(g - 1, (g - 1) % 4)
                if g + 3 < FULL:
                    load_x(g + 3, (g + 3) % 4)
                elif g + 3 == FULL:
                    load_last_x()
            slot = FULL % 4
            act.wait_ge(stored[slot], 16 * (FULL // 4))
            act.wait_ge(stepped, STEPS)
            b = GROUP * (slot % 2)
            nc.scalar.activation(yout[:, slot, 0:LAST_WHOLE, :], bank[:, b:b + LAST_WHOLE, 0:T],
                                 ACT.Sigmoid).then_inc(sig_done, 1)
            nc.scalar.activation(yout[0:N % P, slot, LAST_WHOLE, :], bank[0:N % P, b + LAST_WHOLE, 0:T],
                                 ACT.Sigmoid).then_inc(sig_done, 1)
            store(FULL - 1, (FULL - 1) % 4)
            act.wait_ge(summed, GROUPS)
            act.dma_start(out[FULL * GROUP * P:last_row, :].rearrange("(t p) d -> p t d", p=P),
                          yout[:, slot, 0:LAST_WHOLE, :]).then_inc(stored[slot], 16)
            act.dma_start(out[last_row:N, :], yout[0:N % P, slot, LAST_WHOLE, :]).then_inc(stored[slot], 16)
            for k in range(YS):
                act.wait_ge(stored[k], 16 * len(range(k, GROUPS, YS)) + (16 if k == slot else 0))

        @block.tensor
        def _(pe):
            pe.wait_ge(const_set, 7)
            pe.wait_ge(src_f32, 1)
            for b in range(BLK):
                last = nc.tensor.transpose(bank[:, 6, b * P:(b + 1) * P], src_f[:, b, :], ident[:, :])
            last.then_inc(src_turned, 1)
            pe.wait_ge(w_in, 96)
            for c in range(KD):
                for t in range(KT):
                    last = nc.tensor.transpose(bank[:, 7, c * T + t * P:c * T + (t + 1) * P],
                                               w_nat[:, t, c * P:(c + 1) * P], ident[:, :])
            last.then_inc(w_turned, 1)
            for t in range(KT):
                last = nc.tensor.transpose(bank[:, 5, t * K:(t + 1) * K], qg[:, t * P:(t + 1) * P],
                                           ident[0:K, 0:K])
            last.then_inc(qg_turned, 1)
            pe.wait_ge(q_t_ready, 1)
            pe.wait_ge(b_ready, 1)
            for c in range(KD + 1):
                for t in range(KT):
                    lhs = b_rep[:, t, :] if c == KD else w_nat[:, t, c * P:(c + 1) * P]
                    last = nc.tensor.matmul(bank[:, 4, c * K:(c + 1) * K], lhs, q_t[:, t, :],
                                            start=(t == 0), stop=(t == KT - 1))
            last.then_inc(wq_done, 1)

            def by_step(lhs, rhs, b0, s_sem, m=P, cols=STEPS):
                for n0 in range(0, cols, 512):
                    n1 = min(cols, n0 + 512)
                    for b in range(BLK):
                        last = nc.tensor.matmul(bank[0:m, b0 + n0 // 512, 0:n1 - n0], lhs(b), rhs(b, n0, n1),
                                                start=(b == 0), stop=(b == BLK - 1))
                last.then_inc(s_sem, 1)

            pe.wait_ge(done_ready, 1)
            by_step(lambda b: ones[:, :], lambda b, n0, n1: done[:, b, n0:n1], 0, i_summed)
            pe.wait_ge(sel_ready, 1)
            by_step(lambda b: dst_f[:, b, :], lambda b, n0, n1: sel[:, b, n0:n1], 2, rel_summed)
            pe.wait_ge(ended_ready, 1)
            by_step(lambda b: ones[:, :], lambda b, n0, n1: done[:, b, n0:n1], 0, end_summed, cols=NODES)
            for b in range(BLK):
                last = nc.tensor.transpose(bank[0:1, 6, b * P:(b + 1) * P], s_done[:, b:b + 1], ident[:, :])
            last.then_inc(end_summed, 1)
            pe.wait_ge(tables_ready, 1)

            def tick(t0, k, edge):
                t = t0 + k
                if not edge or 0 <= t < TILES:
                    n = LAST if edge and t == TILES - 1 else P
                    pe.wait_ge(added, t + 1)
                    if not edge or t >= 2:
                        pe.wait_ge(relu_done, t - 1)
                    for c in range(KD):
                        last = nc.tensor.transpose(bank[:, k % 2, c * P:c * P + n], u[0:n, k % 4, c * P:(c + 1) * P],
                                                   ident[0:n, 0:n])
                    last.then_inc(turned, 1)
                if not edge or 1 <= t <= TILES:
                    n = LAST if edge and t == TILES else P
                    pe.wait_ge(relu_done, t)
                    if not edge or t >= 5:
                        pe.wait_ge(p_out, t - 4)
                    for c in range(KD):
                        last = nc.tensor.matmul(bank[0:n, 2 + (k - 1) % 4, 0:NT], msg_t[:, (k - 1) % 4, c, 0:n],
                                                w_all[:, c, :], start=(c == 0), stop=(c == KD - 1))
                    last.then_inc(multiplied, 1)

            stage1(pe, tick)

            pe.wait_ge(p_out, TILES)
            for k in range(K):
                for b in range(BLK):
                    last = nc.tensor.transpose(bank[:, k // 2, (k % 2) * TP + b * P:(k % 2) * TP + (b + 1) * P],
                                               logits[:, b * P:(b + 1) * P, k], ident[:, :])
            last.then_inc(rows_turned, 1)

            def turn_ends(cols, m, count):
                pe.wait_ge(totals_ready, count)
                for side in range(2):
                    for b in range(BLK):
                        last = nc.tensor.transpose(bank[0:m, 5, side * TP + b * P:side * TP + (b + 1) * P],
                                                   cols(b, side), ident[:, :])
                last.then_inc(ends_turned, 1)

            def turn_carries(m, count):
                pe.wait_ge(carries_ready, count)
                for b in range(BLK):
                    for side in range(2):
                        o = (2 * b + side) * C
                        last = nc.tensor.transpose(bank[:, 4, o:o + m], row_b[0:m, 3 + side, b * P:(b + 1) * P],
                                                   ident[0:m, 0:m])
                last.then_inc(carries_turned, 1)

            edge_of = lambda b, side: b * P + (P - 1) * side
            turn_ends(lambda b, side: ends[:, b, side, :], C, 1)
            turn_ends(lambda b, side: tot[:, 0:H, edge_of(b, side)], H, 2)
            turn_carries(H, 1)
            turn_ends(lambda b, side: tot[:, 0:C, edge_of(b, side)], C, 3)
            turn_carries(C, 2)
            pe.wait_ge(c_ready, 1)
            by_step(lambda b: flag[:, 2, b * P:(b + 1) * P], lambda b, n0, n1: sel[:, b, n0:n1], 6, wgt_summed)

            banks, kept = bank[:, :, :].rearrange("p b n -> p (b n)"), p_keep[:, :, :].rearrange("p t d -> p (t d)")

            def steps(s0, n):
                load = lambda table, top: nc.values_load_multi_w_load_instructions(
                    table[:, bass.ds(s0, n)], engines=[pe.engine], min_val=0, max_val=top)[1]
                for k, (o, r) in enumerate(zip(load(walk_bank, 7 * 512), load(walk_p, (RING - 1) * T))):
                    pe.wait_ge(spread_ready, s0 + k + 1)
                    nc.tensor.matmul(banks[:, bass.ds(o, T)], spread[:, k % SPREADS, :], kept[:, bass.ds(r, T)],
                                     start=False, stop=True, skip_group_check=True).then_inc(stepped, 1)

            pe.wait_ge(wgt_ready, 1)
            for b in range(8):
                nc.tensor.matmul(bank[:, b, 0:T], zeros[:, 0:P], zeros[:, 0:T], start=True, stop=True)
            with pe.Fori(0, STEPS // UNROLL) as n:
                steps(n * UNROLL, UNROLL)
            steps(STEPS - STEPS % UNROLL, STEPS % UNROLL)

        @block.vector
        def _(dve):
            steps = [0]

            def then(ins):
                steps[0] += 1
                ins.then_inc(dve_step, 1)
                dve.wait_ge(dve_step, steps[0])

            v = nc.vector
            dve.wait_ge(const_set, 7)
            dve.wait_ge(src_in, 48)
            v.tensor_copy(src_f, src_i).then_inc(src_f32, 1)
            v.tensor_copy(step_f[:, :], step_i)
            v.tensor_copy(tile_f[:, :], tile_i[:, :])
            dve.wait_ge(dst_in, 48)
            then(v.tensor_copy(dst_f[:, :, :], dst_i))
            dve.wait_ge(src_turned, 1)
            v.tensor_copy(idx[:, :], bank[:, 6, 0:TP]).then_inc(idx_ready, 1)
            dve.wait_ge(w_in, 96)
            v.tensor_copy(b_rep, b_col.unsqueeze(2).broadcast_to([P, KT, P])).then_inc(b_ready, 1)
            dve.wait_ge(w_turned, 1)
            v.tensor_copy(w_all[:, :, 0:T], bank[:, 7, :].rearrange("p (c t) -> p c t", c=KD))
            dve.wait_ge(qg_turned, 1)
            v.tensor_copy(q_t, bank[:, 5, 0:KT * K].rearrange("p (c k) -> p c k", c=KT)).then_inc(q_t_ready, 1)
            then(v.tensor_scalar(node_of[:, :], dst_f[:, :, P - 1], float(N - 1), None, ALU.min))
            then(v.tensor_copy(node_i[:, :], node_of[:, :]))
            then(v.tensor_scalar(node_i[:, :], node_i[:, :], SHIFT, None, ALU.arith_shift_right))
            then(v.tensor_copy(node_of[:, :], node_i[:, :]))
            then(v.tensor_tensor(s_done[:, :], node_of[:, :], tile_f[:, :], ALU.add))
            for b in range(BLK):
                ins = v.tensor_scalar(done[:, b, :], step_f[:, :], s_done[:, b:b + 1], None, ALU.is_gt)
            then(ins)
            dve.sem_inc(done_ready, 1)
            dve.wait_ge(wq_done, 1)
            v.tensor_copy(w_all[:, :, T:NT], bank[:, 4, 0:KD * K].rearrange("p (c k) -> p c k", c=KD))
            v.tensor_copy(bias[:, T:NT], bank[:, 4, KD * K:(KD + 1) * K]).then_inc(w_ready, 1)
            dve.wait_ge(i_summed, 1)
            v.tensor_copy(i_of[:, 0:512], bank[:, 0, :])
            then(v.tensor_copy(i_of[:, 512:STEPS], bank[:, 1, 0:STEPS - 512]))
            for b in range(BLK):
                ins = v.tensor_scalar(sel[:, b, :], i_of, tile_f[:, b:b + 1], None, ALU.is_equal)
            ins.then_inc(sel_ready, 1)
            for b in range(BLK):
                ins = v.tensor_scalar(done[:, b, 0:NODES], step_f[:, 0:NODES], node_of[:, b:b + 1], None, ALU.is_ge)
            ins.then_inc(ended_ready, 1)
            then(v.scalar_tensor_tensor(j_of[:, 0:STEPS], i_of, -1.0, step_f[:, :], ALU.mult, ALU.add))
            dve.wait_ge(rel_summed, 1)
            v.scalar_tensor_tensor(rel[:, 0:512], j_of[:, 0:512], -float(P), bank[:, 2, :], ALU.mult, ALU.add)
            then(v.scalar_tensor_tensor(rel[:, 512:STEPS], j_of[:, 512:STEPS], -float(P),
                                        bank[:, 3, 0:STEPS - 512], ALU.mult, ALU.add))
            dve.wait_ge(end_summed, 2)
            tile, slot, j_int = done[:, 0, 0:STEPS], done[:, 1, 0:STEPS], rel_tmp.bitcast(I32)
            then(v.tensor_copy(j_int, j_of[:, 0:STEPS]))
            v.tensor_scalar(walk_bank, j_int[0:1, :], 7, 9, ALU.bitwise_and, ALU.logical_shift_left)
            then(v.tensor_scalar(j_int[64:65, :], j_int[64:65, :], 2, None, ALU.logical_shift_right))
            v.tensor_scalar(need_bank[:, 0:FOURS], j_int[64:65, 3:4 * FOURS:4], 1.0, None, ALU.add)
            then(v.tensor_scalar(tile, i_of, float(TILES - 1), None, ALU.min))
            v.tensor_scalar(need_p[:, 0:FOURS], tile[32:33, 3:4 * FOURS:4], 1.0, None, ALU.add)
            then(v.tensor_scalar(slot, tile, float(RING), -float(RING), ALU.is_ge, ALU.mult))
            then(v.tensor_tensor(slot, slot, tile, ALU.add))
            v.tensor_scalar(walk_p, slot[32:33, :], float(T), None, ALU.mult)
            node = rel_tmp[96:97, 0:NODES]
            then(v.scalar_tensor_tensor(node, bank[96:97, 0, 0:NODES], 1.0, step_f[96:97, 0:NODES],
                                        ALU.add, ALU.add))
            v.tensor_scalar(node_end[:, 0:NODES], node, float(STEPS), None, ALU.min)
            then(v.tensor_scalar(tile_end[:, 0:TP], bank[0:1, 6, 0:TP], 1.0, float(STEPS), ALU.add, ALU.min))
            dve.sem_inc(tables_ready, 1)

            def tick(t0, k, edge):
                t = t0 + k
                n, m = t + LEAD, (k + LEAD) % BODY
                ahead = not edge or 0 <= n < TILES
                na = LAST if edge and n == TILES - 1 else P
                if ahead:
                    dve.wait_ge(gathered[m], (t0 if not edge else 0) + 16 * ((k + LEAD) // BODY) + 16)
                    v.bn_stats(stats[0:na, m, :], xg[0:na, m, :]).then_inc(stats_done, 1)
                if not edge or 0 <= t < TILES:
                    r = LAST if edge and t == TILES - 1 else P
                    q = (k // 4) % 4
                    dve.wait_ge(ln_done, t + 1)
                    more = 16 if edge and t >= BODIES * BODY else 0
                    dve.wait_ge(ea_in[q], (t0 if not edge else 0) + 16 * (k // BODY) + 16 + more)
                    v.tensor_tensor(u[0:r, k % 4, :], u[0:r, k % 4, :], ea[0:r, k % BODY, :],
                                    ALU.add).then_inc(added, 1)
                if not edge or LAG <= t < TILES + LAG:
                    e = t - LAG
                    b = 2 + (k - LAG) % 4
                    r = LAST if edge and e == TILES - 1 else P
                    late = (e >= RING) if edge else t0_late[0]
                    if late:
                        slot = RING + (k - LAG - RING) % STAGE
                        if not edge or e >= RING + STAGE:
                            w = (2 * t0 - 2 * SPLIT * BODY + 16 * (k // 8)) if not edge else 16 * ((e - RING) // 8)
                            w = w + 16
                            dve.wait_ge(spilled[(slot - RING) // 4], w)
                        to = p_keep[:, slot:slot + 1, :].rearrange("p t d -> p (t d)")
                        if r < P:
                            v.memset(to, 0.0).then_inc(padded, 1)
                            dve.wait_ge(padded, 1)
                    else:
                        to = p_keep[:, bass.ds(e, 1), :].rearrange("p t d -> p (t d)")
                    dve.wait_ge(multiplied, e + 1)
                    v.tensor_tensor(logits[0:r, bass.ds(e, 1), :].rearrange("p t k -> p (t k)"), bank[0:r, b, T:NT],
                                    bias[0:r, T:NT], ALU.add)
                    v.tensor_tensor(to[0:r], bank[0:r, b, 0:T], bias[0:r, 0:T], ALU.add).then_inc(p_out, 1)
                if k % 4 == (3 - LEAD) % 4 and ahead:
                    dve.wait_ge(stats_done, n + 1)
                    dve.sem_inc(stats_seen, 1)
                    for a in range(4):
                        na = LAST if edge and n - 3 + a == TILES - 1 else P
                        v.bn_aggr(mv[0:na, m - 3 + a, :], stats[0:na, m - 3 + a, :]).then_inc(mv_done, 1)
                if k % 4 == 3:
                    q = t + LEAD - 5
                    if not edge or 0 <= q < TILES:
                        m4 = (k + LEAD - 5) % BODY
                        c = (t0 // 4) + (k + LEAD - 5) // 4 + 1
                        dve.wait_ge(std_done, c)
                        v.reciprocal(rstd[:, m4:m4 + 4], rstd[:, m4:m4 + 4]).then_inc(rstd_done, 1)
                        dve.wait_ge(rstd_done, c)
                        v.scalar_tensor_tensor(negmr[:, m4:m4 + 4], mv[:, m4:m4 + 4, 0], -1.0, rstd[:, m4:m4 + 4],
                                               ALU.mult, ALU.mult).then_inc(norm_ready, 1)

            stage1(dve, tick)

            same, same_next, end, in_first, in_last, neg = (flag[:, n, :] for n in range(6))
            per_blk = lambda a: a.rearrange("p (b e) -> p b e", b=BLK)
            dst_rows = dst_f[:, :, :].rearrange("p b e -> p (b e)")
            dve.wait_ge(turned, TILES)
            dve.wait_ge(multiplied, TILES)
            v.memset(same, 0.0)
            then(v.memset(same_next, 0.0))
            v.tensor_tensor(per_blk(same)[:, :, 1:P], dst_f[:, :, 1:P], dst_f[:, :, 0:P - 1], ALU.is_equal)
            then(v.tensor_tensor(per_blk(same_next)[:, :, 0:P - 1], dst_f[:, :, 1:P], dst_f[:, :, 0:P - 1],
                                 ALU.is_equal))
            v.tensor_scalar(end, same_next, -1.0, 1.0, ALU.mult, ALU.add)
            v.tensor_scalar(neg, same, 1.0, BIG, ALU.subtract, ALU.mult)
            for b in range(BLK):
                sl = slice(b * P, (b + 1) * P)
                v.tensor_scalar(in_first[:, sl], dst_f[:, b, :], dst_f[:, b, 0:1], None, ALU.is_equal)
                v.tensor_scalar(in_last[:, sl], dst_f[:, b, :], dst_f[:, b, P - 1:P], None, ALU.is_equal)
                for side in range(2):
                    c = (P - 1) * side
                    ins = v.tensor_copy(ends[:, b, side, :], dst_f[:, b, c:c + 1].broadcast_to([P, C]))
            then(ins)
            dve.sem_inc(totals_ready, 1)
            v.memset(val[:, 2 * H, :], 1.0)
            dve.wait_ge(rows_turned, 1)
            for g in range(K // 2):
                ins = v.tensor_copy(val[:, 2 * g:2 * g + 2, :], bank[:, g, :].rearrange("p (k e) -> p k e", k=2))
            then(ins)
            first_d, last_d, cont, whole_t, fwd_keep, bwd_keep, first_v = (row_a[:, n, :] for n in range(7))
            last_v, keep, give, from_left, from_right, cneg = (row_b[:, n, :] for n in range(6))
            dve.wait_ge(ends_turned, 1)
            v.tensor_copy(first_d[:, 0:TP], bank[0:C, 5, 0:TP])
            v.memset(cont, 0.0)
            v.memset(fwd_keep, 0.0)
            v.memset(bwd_keep, 0.0)
            then(v.tensor_copy(last_d[:, 0:TP], bank[0:C, 5, TP:2 * TP]))
            v.tensor_tensor(cont[:, 1:TP], first_d[:, 1:TP], last_d[:, 0:TP - 1], ALU.is_equal)
            then(v.tensor_tensor(whole_t[:, 0:TP], first_d[:, 0:TP], last_d[:, 0:TP], ALU.is_equal))
            v.tensor_tensor(fwd_keep[:, 1:TP], cont[:, 1:TP], whole_t[:, 0:TP - 1], ALU.mult)
            v.tensor_tensor(bwd_keep[:, 0:TP - 1], cont[:, 1:TP], whole_t[:, 1:TP], ALU.mult)
            then(v.tensor_scalar(cneg, cont, 1.0, BIG, ALU.subtract, ALU.mult))

            def over_edges(k, ops, data0):
                for n in range(k):
                    ins = v.tensor_tensor_scan(run[:, n, :], data0, val[:, n, :], 0.0, *ops)
                then(ins)
                then(v.tensor_tensor(run[:, 0:k, :], run[:, 0:k, :], end.unsqueeze(1).broadcast_to([P, k, RW]),
                                     ALU.mult))
                for n in range(k):
                    ins = v.tensor_tensor_scan(tot[:, n, ::-1], same_next[:, ::-1], run[:, n, ::-1], 0.0,
                                               ALU.mult, ALU.add)
                then(ins)
                dve.sem_inc(totals_ready, 1)

            def over_tiles(k, ops, is_max, count):
                dve.wait_ge(ends_turned, count + 1)
                v.tensor_copy(first_v[0:k, 0:TP], bank[0:k, 5, 0:TP])
                then(v.tensor_copy(last_v[0:k, 0:TP], bank[0:k, 5, TP:2 * TP]))
                for side in range(2):
                    r = slice(0, k)
                    here = slice(1, TP) if side == 0 else slice(0, TP - 1)
                    there = slice(0, TP - 1) if side == 0 else slice(1, TP)
                    keeps = (fwd_keep, bwd_keep)[side]
                    gives = (last_v, first_v)[side]
                    to = (from_left, from_right)[side]
                    then(v.memset(give[r, 0:TP], -BIG if is_max else 0.0))
                    then(v.tensor_tensor(give[r, here], cont[r, 1:TP], gives[r, there], ALU.mult))
                    if is_max:
                        then(v.tensor_tensor(give[r, here], give[r, here], cneg[r, 1:TP], ALU.add))
                        then(v.tensor_scalar(keep[r, 0:TP], keeps[r, 0:TP], 1.0, BIG, ALU.subtract, ALU.mult))
                        d0 = keep[r, 0:TP]
                    else:
                        d0 = keeps[r, 0:TP]
                    back = slice(None, None, -1 if side else 1)
                    then(v.tensor_tensor_scan(to[r, 0:TP][:, back], d0[:, back], give[r, 0:TP][:, back],
                                              -BIG if is_max else 0.0, *ops))
                dve.sem_inc(carries_ready, 1)
                dve.wait_ge(carries_turned, count)
                then(v.tensor_copy(carry[:, :, :, 0:k], bank[:, 4, 0:BLK * 2 * C].rearrange(
                    "p (b s k) -> p b s k", b=BLK, s=2)[:, :, :, 0:k]))
                for side in range(2):
                    mask = (in_first, in_last)[side]
                    if is_max:
                        then(v.tensor_scalar(neg, mask, 1.0, BIG, ALU.subtract, ALU.mult))
                        mask = neg
                    for n in range(k):
                        for b in range(BLK):
                            sl = slice(b * P, (b + 1) * P)
                            ins = v.scalar_tensor_tensor(tot[:, n, sl], mask[:, sl], carry[:, b, side, n:n + 1],
                                                         tot[:, n, sl], ALU.add if is_max else ALU.mult,
                                                         ALU.max if is_max else ALU.add)
                    then(ins)

            over_edges(H, (ALU.add, ALU.max), neg)
            over_tiles(H, (ALU.add, ALU.max), True, 1)
            v.tensor_tensor(val[:, 0:H, :], val[:, 0:H, :], tot[:, 0:H, :], ALU.subtract).then_inc(diff_ready, 1)
            dve.wait_ge(exp_done, 1)
            over_edges(C, (ALU.mult, ALU.add), same)
            over_tiles(C, (ALU.mult, ALU.add), False, 2)
            over_h = lambda a: a.unsqueeze(1).broadcast_to([P, H, RW])
            then(v.tensor_scalar(run[:, 2 * H, :], tot[:, 2 * H, :], 1.0, None, ALU.max))
            then(v.reciprocal(run[:, 2 * H, :], run[:, 2 * H, :]))
            then(v.tensor_tensor(run[:, H:K, :], tot[:, H:K, :], over_h(run[:, 2 * H, :]), ALU.mult))
            for h in range(H):
                ins = v.tensor_scalar(run[:, H + h, :], run[:, H + h, :], bg_b[:, h:h + 1], None, ALU.add)
            then(ins)
            then(v.tensor_tensor(run[:, 0:2, :], run[:, H:H + 2, :], run[:, H + 2:K, :], ALU.max))
            then(v.tensor_tensor(run[:, 0, :], run[:, 0, :], run[:, 1, :], ALU.max))
            v.tensor_tensor(run[:, H:K, :], run[:, H:K, :], over_h(run[:, 0, :]), ALU.subtract).then_inc(diff_ready, 1)
            then(v.tensor_scalar(tot[:, 0:H, :], tot[:, 0:H, :], 1e-9, None, ALU.max))
            then(v.reciprocal(tot[:, 0:H, :], tot[:, 0:H, :]))
            then(v.tensor_tensor(tot[:, 0:H, :], tot[:, 0:H, :], val[:, 0:H, :], ALU.mult))
            dve.wait_ge(exp_done, 2)
            v.tensor_tensor(tot[:, 0:H, :], tot[:, 0:H, :], run[:, H:K, :], ALU.mult)
            then(v.tensor_tensor(run[:, 0:2, :], run[:, H:H + 2, :], run[:, H + 2:K, :], ALU.add))
            then(v.tensor_tensor(run[:, 0, :], run[:, 0, :], run[:, 1, :], ALU.add))
            then(v.reciprocal(run[:, 0, :], run[:, 0, :]))
            then(v.tensor_tensor(tot[:, 0:2, :], tot[:, 0:2, :], tot[:, 2:4, :], ALU.add))
            then(v.tensor_tensor(tot[:, 0, :], tot[:, 0, :], tot[:, 1, :], ALU.add))
            then(v.tensor_tensor(flag[:, 2, :], tot[:, 0, :], run[:, 0, :], ALU.mult))
            dve.sem_inc(c_ready, 1)
            dve.wait_ge(wgt_summed, 1)
            v.tensor_copy(wgt[:, 0:512], bank[:, 6, :])
            then(v.tensor_copy(wgt[:, 512:STEPS], bank[:, 7, 0:STEPS - 512]))
            dve.sem_inc(wgt_ready, 1)

            def spread_out(s, slot, wait=True):
                if wait:
                    dve.wait_ge(stepped, s - SPREADS + 1)
                v.tensor_scalar(spread[:, slot, :], step_f[:, 0:P], rel[:, bass.ds(s, 1)], wgt[:, bass.ds(s, 1)],
                                ALU.is_equal, ALU.mult).then_inc(spread_ready, 1)

            def fours(n0, count):
                load = lambda table, top: nc.values_load_multi_w_load_instructions(
                    table[:, bass.ds(n0, count)], engines=[dve.engine], min_val=1, max_val=top)[1]
                for n, (tiles, groups) in enumerate(zip(load(need_p, TILES), load(need_bank, GROUPS))):
                    dve.wait_ge(p_ready, tiles)
                    dve.wait_ge(bank_zero, groups)
                    for k in range(4):
                        spread_out(4 * (n0 + n) + k, (4 * n + k) % SPREADS)

            for s in range(SPREADS):
                spread_out(s, s, False)
            with dve.Fori(0, (FOURS - 2) // 8) as n:
                fours(8 * n + SPREADS // 4, 8)
            dve.wait_ge(p_ready, TILES)
            dve.wait_ge(bank_zero, GROUPS)
            for s in range(4 * FOURS, STEPS):
                spread_out(s, s % SPREADS)


_INS = ['x', 'src', 'dst', 'edge_attr_256', 'L0_gnn_W_fc', 'L0_gnn_b_fc', 'L0_gnn_Q', 'L0_gnn_Wg', 'L0_gnn_bg']
_OUTS = [((50000, 256), 'float32')]


def kernel(**inputs):
    import numpy as _np
    import concourse.bacc as _bacc
    from concourse import mybir as _mybir
    from concourse.bass_utils import run_bass_kernel_spmd as _run

    nc = _bacc.Bacc("TRN2", target_bir_lowering=False, num_devices=1)
    arrays, args = {}, []
    for name in _INS:
        a = _np.ascontiguousarray(inputs[name])
        arrays[f"in_{name}_dram"] = a
        args.append(nc.dram_tensor(f"in_{name}_dram", a.shape, _mybir.dt.from_np(a.dtype), kind="ExternalInput").ap())
    for i, (shape, dtype) in enumerate(_OUTS):
        dt = _mybir.dt.from_np(_np.dtype(dtype))
        args.append(nc.dram_tensor(f"out_{i}_dram", shape, dt, kind="ExternalOutput").ap())
    gnn_layer(nc, *args)
    r = _run(nc, [arrays], core_ids=[0])
    return r.results[0]["out_0_dram"]
```

```python
from contextlib import ExitStack

import concourse.bass as bass
from concourse import mybir

F32 = mybir.dt.float32
I32 = mybir.dt.int32
ALU = mybir.AluOpType
ACT = mybir.ActivationFunctionType
AX = mybir.AxisListType

P = 128
BIG = 1.0e30
LN_EPS = 1e-5
BODY = 16
LEAD = 6
LAG = 4


def gnn_layer(nc, x, src, dst, edge_attr, w_fc, b_fc, q_w, g_w, b_g, out):
    N, D = x.shape
    E = src.shape[0]
    T = w_fc.shape[0]
    H = q_w.shape[0]
    K = 2 * H
    C = 2 * H + 1
    KD, KT = D // P, T // P
    TILES = -(-E // P)
    LAST = E - (TILES - 1) * P
    BLK = -(-TILES // P)
    TP = BLK * P
    NODES = -(-N // P)
    NP1 = NODES + 1
    PAD = 1 << 16
    SHIFT = P.bit_length() - 1
    NT = T + K
    BODIES = TILES // BODY
    SPLIT = 8
    RING = SPLIT * BODY - LAG
    STAGE = 8
    SPILL = TILES - RING
    assert RING % 4 == 0 and SPILL % 4 == 0 and SPILL <= RING and (RING + LAG) % BODY == 0

    GROUP = 4
    GROUPS = -(-NODES // GROUP)
    FULL = N // (GROUP * P)
    assert GROUPS == FULL + 1 and FULL % 2 == 1
    LAST_WHOLE = (N - FULL * GROUP * P) // P
    LOOPED = (FULL - 3) // 4 * 4
    XS, YS = 4, 4
    assert FULL % 4 == 1 and LAST_WHOLE == 2 and N % P and LOOPED + 3 < FULL

    scratch = nc.dram_tensor("p_spill", [SPILL * P, T], F32).ap()

    with ExitStack() as ctx:
        def sb(name, shape, dt=F32):
            return ctx.enter_context(nc.sbuf_tensor(name, shape, dt))

        def sem(name):
            return ctx.enter_context(nc.semaphore(name))

        bank = ctx.enter_context(nc.psum_tensor("bank", [P, 8, 512], F32))

        p_keep = sb("p_keep", [P, RING + STAGE, T])
        arena = sb("arena", [P, 10240])
        logits = sb("logits", [P, TP, K])
        w_all = sb("w_all", [P, KD, NT])
        bias = sb("bias", [P, NT])
        ident = sb("ident", [P, P])
        ones = sb("ones", [P, P])
        count_f = sb("count_f", [P, NP1])
        lo = sb("lo", [P, NP1])
        rel = sb("rel", [P, 2, NODES])
        wgt = sb("wgt", [P, 2, NODES])
        rel_x = sb("rel_x", [P, TP])
        wgt_x = sb("wgt_x", [P, TP])
        dst_f = sb("dst_f", [P, BLK, P])
        idx = sb("idx", [P, TP], I32)
        idx_slot = sb("idx_slot", [P, BODY], I32)
        spread = sb("spread", [P, 2 * GROUP, P])
        stats = sb("stats", [P, BODY, 6])
        mv = sb("mv", [P, BODY, 2])
        rstd = sb("rstd", [P, BODY])
        negmr = sb("negmr", [P, BODY])
        eps = sb("eps", [P, 1])
        bg_b = sb("bg_b", [P, H])
        tile_f = sb("tile_f", [P, BLK])
        tile_i = sb("tile_i", [P, BLK], I32)
        spread_x = sb("spread_x", [P, P])
        node_of = sb("node_of", [P, BLK])
        node_i = sb("node_i", [P, BLK], I32)
        by_tile = sb("by_tile", [P, TP], I32)
        free_fixed, free_extra, slot_of, ordinal = (by_tile[32 * n:32 * n + 1, :] for n in range(4))
        by_node = sb("by_node", [P, NP1], I32)
        lo_i, extras_of, slots_of, flags_of = (by_node[32 * n:32 * n + 1, :] for n in range(4))
        more = sb("more", [P, NP1], I32)
        extras_by, needs_of, wants_of = more[0:1, 0:GROUPS], more[32:33, 0:GROUPS], more[64:65, :]

        o = 0
        xg = arena[:, o:o + BODY * D].rearrange("p (t d) -> p t d", d=D); o += BODY * D
        ea = arena[:, o:o + BODY * D].rearrange("p (t d) -> p t d", d=D); o += BODY * D
        u = arena[:, o:o + 4 * D].rearrange("p (t d) -> p t d", d=D); o += 4 * D
        msg_t = arena[:, o:o + 4 * D].rearrange("p (t c e) -> p t c e", c=KD, e=P); o += 4 * D
        assert o <= 10240
        o = 0
        RW = BLK * P
        val = arena[:, o:o + C * RW].rearrange("p (k e) -> p k e", k=C); o += C * RW
        run = arena[:, o:o + C * RW].rearrange("p (k e) -> p k e", k=C); o += C * RW
        tot = arena[:, o:o + C * RW].rearrange("p (k e) -> p k e", k=C); o += C * RW
        flag = arena[:, o:o + 6 * RW].rearrange("p (k e) -> p k e", k=6); o += 6 * RW
        row_b = arena[0:C, o:o + 6 * (TP + 1)].rearrange("p (k t) -> p k t", k=6); o += 6 * (TP + 1)
        carry = arena[:, o:o + BLK * 2 * C].rearrange("p (b s k) -> p b s k", b=BLK, s=2); o += BLK * 2 * C
        assert o <= 10240
        row_a = logits[0:C, :, :].rearrange("p t k -> p (t k)")[:, 0:7 * (TP + 1)].rearrange("p (k t) -> p k t", k=7)
        sel_1 = arena[:, C * RW:C * RW + 2 * BLK * NODES].rearrange("p (w b j) -> p w b j", w=2, b=BLK)
        assert 2 * BLK * NODES <= C * RW
        ends = tot[:, 0, 0:BLK * 2 * C].rearrange("p (b s k) -> p b s k", b=BLK, s=2)
        xin = arena[:, 0:XS * GROUP * D].rearrange("p (s q d) -> p s q d", s=XS, q=GROUP)
        yout = arena[:, XS * GROUP * D:(XS + YS) * GROUP * D].rearrange("p (s q d) -> p s q d", s=YS, q=GROUP)
        tail = p_keep[:, RING - 30:RING, :].rearrange("p t d -> p (t d)")
        o = 0
        w_nat = tail[:, o:o + KT * D].rearrange("p (c d) -> p c d", c=KT); o += KT * D
        b_rep = tail[:, o:o + KT * P].rearrange("p (c e) -> p c e", c=KT); o += KT * P
        q_t = tail[:, o:o + KT * K].rearrange("p (c k) -> p c k", c=KT); o += KT * K
        qg = tail[0:K, o:o + T]; o += T
        b_col = tail[:, o:o + KT]; o += KT
        before = tail[:, o:o + BLK * NP1].rearrange("p (b j) -> p b j", b=BLK); o += BLK * NP1
        sel_0 = tail[:, o:o + 2 * BLK * NODES].rearrange("p (w b j) -> p w b j", w=2, b=BLK); o += 2 * BLK * NODES
        diag = tail[:, o:o + TP].rearrange("p (b t) -> p b t", b=BLK); o += TP
        count_i = tail[:, o:o + NP1].bitcast(I32); o += NP1
        tmp = [tail[:, o + n * NP1:o + (n + 1) * NP1] for n in range(5)]; o += 5 * NP1
        src_f = tail[:, o:o + TP].rearrange("p (b e) -> p b e", b=BLK); o += TP
        assert o <= 30 * T
        src_i = p_keep[:, RING - 32, :].rearrange("p (b e) -> p b e", b=BLK).bitcast(I32)
        dst_i = p_keep[:, RING - 31, :].rearrange("p (b e) -> p b e", b=BLK).bitcast(I32)

        pads_set = sem("pads_set")
        src_in, dst_in, w_in = sem("src_in"), sem("dst_in"), sem("w_in")
        const_set = sem("const_set")
        src_f32, src_turned, idx_ready = sem("src_f32"), sem("src_turned"), sem("idx_ready")
        w_turned, qg_turned, q_t_ready, b_ready = sem("w_turned"), sem("qg_turned"), sem("q_t_ready"), sem("b_ready")
        wq_done, w_ready = sem("wq_done"), sem("w_ready")
        before_ready, lo_summed, sel_ready = sem("before_ready"), sem("lo_summed"), sem("sel_ready")
        rel_summed = sem("rel_summed")
        tables_ready = sem("tables_ready")
        dve_step, pool_step = sem("dve_step"), sem("pool_step")
        idx_copied, idx_seen, stats_seen = sem("idx_copied"), sem("idx_seen"), sem("stats_seen")
        gathered = [sem(f"gathered{k}") for k in range(BODY)]
        ea_in = [sem(f"ea_in{k}") for k in range(4)]
        stats_done, mv_done = sem("stats_done"), sem("mv_done")
        std_done, rstd_done, norm_ready = sem("std_done"), sem("rstd_done"), sem("norm_ready")
        ln_done, added, turned, relu_done = sem("ln_done"), sem("added"), sem("turned"), sem("relu_done")
        multiplied, p_out, padded = sem("multiplied"), sem("p_out"), sem("padded")
        spilled = [sem("spilled0"), sem("spilled1")]
        rows_turned, ends_turned, carries_ready = sem("rows_turned"), sem("ends_turned"), sem("carries_ready")
        totals_ready, carries_turned = sem("totals_ready"), sem("carries_turned")
        diff_ready, exp_done = sem("diff_ready"), sem("exp_done")
        c_ready, wgt_summed, wgt_ready = sem("c_ready"), sem("wgt_summed"), sem("wgt_ready")
        spread_ready, stepped = sem("spread_ready"), sem("stepped")
        extra_ready, extra_done = sem("extra_ready"), sem("extra_done")
        p_ready, reloaded = sem("p_ready"), sem("reloaded")
        sig_done, summed = sem("sig_done"), sem("summed")
        x_in = [sem(f"x_in{k}") for k in range(XS)]
        stored = [sem(f"stored{k}") for k in range(YS)]

        t0_late = [False]

        def stage1(eng, tick):
            for k in range(-LEAD, BODY):
                tick(0, k, True)
            for a, b in ((1, SPLIT), (SPLIT, BODIES - 1)):
                t0_late[0] = a == SPLIT
                with eng.Fori(a, b) as body:
                    t0 = body * BODY
                    for k in range(BODY):
                        tick(t0, k, False)
            for k in range((BODIES - 1) * BODY, TILES + LAG):
                tick(0, k, True)

        in_range = "the extras of node tile j are the tiles lo[j] + 2 .. lo[j + 1], and lo is at most TILES - 1"

        block = ctx.enter_context(nc.Block())

        @block.sync
        def _(sp):
            sp.wait_ge(pads_set, 2)
            for half in range(2):
                sp.sem_inc(spilled[half], 16)
            for dram, tile, done_ in ((src, src_i, src_in), (dst, dst_i, dst_in)):
                whole = (TILES - 1) * P
                sp.dma_start(tile[:, 0, :], dram[0:P * P].rearrange("(t e) -> t e", e=P)).then_inc(done_, 16)
                sp.dma_start(tile[0:TILES - 1 - P, 1, :],
                             dram[P * P:whole].rearrange("(t e) -> t e", e=P)).then_inc(done_, 16)
                sp.dma_start(tile[TILES - 1 - P:TILES - P, 1, 0:LAST],
                             dram[whole:E].rearrange("(t e) -> t e", t=1)).then_inc(done_, 16)
            sp.dma_start(w_nat, w_fc.rearrange("(c p) d -> p c d", p=P)).then_inc(w_in, 16)
            sp.dma_start(qg[0:H, :], q_w).then_inc(w_in, 16)
            sp.dma_start(qg[H:K, :], g_w).then_inc(w_in, 16)
            with nc.allow_non_contiguous_dma(reason="one column of biases, once"):
                sp.dma_start(b_col, b_fc.rearrange("(c p) -> p c", p=P)).then_inc(w_in, 16)
            sp.dma_start(bias[:, 0:T], b_fc.rearrange("(a n) -> a n", a=1).broadcast_to([P, T])).then_inc(w_in, 16)
            sp.dma_start(bg_b[:, :], b_g.rearrange("(a n) -> a n", a=1).broadcast_to([P, H])).then_inc(w_in, 16)

            ea_rows = edge_attr[0:(TILES - 1) * P, :].rearrange("(t p) d -> p t d", p=P)

            def load_ea(t0, quad, first=False):
                if not first:
                    sp.wait_ge(added, t0 + 4 * quad - BODY + 4)
                sp.dma_start(ea[:, 4 * (quad % 4):4 * (quad % 4) + 4, :],
                             ea_rows[:, bass.ds(t0 + 4 * quad, 4), :]).then_inc(ea_in[quad % 4], 16)

            for quad in range(4):
                load_ea(0, quad, True)
            with sp.Fori(1, SPLIT) as body:
                t0 = body * BODY
                for quad in range(4):
                    load_ea(t0, quad)

            def spill(n4, half):
                sp.wait_ge(p_out, RING + n4 + 4)
                sp.dma_start(scratch[bass.ds(n4 * P, 4 * P), :].rearrange("(t p) d -> p t d", p=P),
                             p_keep[:, RING + 4 * half:RING + 4 * half + 4, :]).then_inc(spilled[half], 16)

            with sp.Fori(SPLIT, BODIES) as body:
                t0 = body * BODY
                for quad in range(4):
                    load_ea(t0, quad)
                    spill(t0 + 4 * quad - SPLIT * BODY, quad % 2)
            t0 = BODIES * BODY
            sp.wait_ge(added, t0 - BODY + 4)
            sp.dma_start(ea[:, 0:3, :], ea_rows[:, t0:t0 + 3, :]).then_inc(ea_in[0], 16)
            sp.dma_start(ea[0:LAST, 3, :], edge_attr[(TILES - 1) * P:E, :]).then_inc(ea_in[0], 16)
            n4 = t0 - SPLIT * BODY
            while n4 < SPILL:
                spill(n4, (n4 // 4) % 2)
                n4 += 4
            for half in range(2):
                sp.wait_ge(spilled[half], 16 + 16 * len(range(half, SPILL // 4, 2)))

            sp.wait_ge(tables_ready, 1)
            sp.wait_ge(c_ready, 1)
            sp.sem_inc(p_ready, RING)

            def reload(n, slots):
                fixed_steps = sp.value_load(free_fixed[:, bass.ds(n, 1)], min_val=1, max_val=2 * NODES + 8)
                extra_steps = sp.value_load(free_extra[:, bass.ds(n, 1)], min_val=1, max_val=TP + 1)
                sp.wait_ge(stepped, fixed_steps)
                sp.wait_ge(extra_done, extra_steps)
                for slot in slots:
                    sp.dma_start(p_keep[:, bass.ds(slot, 1), :].rearrange("p t d -> p (t d)"),
                                 scratch[bass.ds(n * P, P), :]).then_inc(reloaded, 16)

            reload(0, (0, RING))
            sp.wait_ge(reloaded, 32)
            sp.sem_inc(p_ready, 1)
            with sp.Fori(1, SPILL) as n:
                reload(n, (n,))
                sp.wait_ge(reloaded, 16 * n + 32)
                sp.sem_inc(p_ready, 1)

        @block.gpsimd
        def _(pool):
            pool.memset(src_i, 0).then_inc(pads_set, 1)
            pool.memset(dst_i, PAD).then_inc(pads_set, 1)
            pool.memset(ident[:, :], 0.0).then_inc(pool_step, 1)
            pool.wait_ge(pool_step, 1)
            pool.affine_select(out=ident[:, :], in_=ident[:, :], compare_op=ALU.not_equal, fill=1.0, base=0,
                               pattern=[[-1, P]], channel_multiplier=1).then_inc(const_set, 1)
            pool.memset(ones[:, :], 1.0).then_inc(const_set, 1)
            pool.iota(count_i, pattern=[[1, NP1]], base=0, channel_multiplier=0).then_inc(const_set, 1)
            pool.iota(tile_i[:, :], pattern=[[P, BLK]], base=0, channel_multiplier=1).then_inc(const_set, 1)
            pool.memset(eps[:, :], LN_EPS).then_inc(const_set, 1)
            pool.memset(logits[:, TILES - 1:TP, :], 0.0).then_inc(const_set, 1)
            pool.wait_ge(idx_ready, 1)

            def gather(t0, k, n=P, first=False):
                if not first:
                    pool.wait_ge(ln_done, t0 + k - BODY + 1)
                pool.tensor_copy(idx_slot[:, k:k + 1], idx[:, bass.ds(t0 + k, 1)]).then_inc(idx_copied, 1)
                pool.wait_ge(idx_copied, t0 + k + 1)
                pool.sem_inc(idx_seen, 1)
                pool.indirect_dma_start(out=xg[0:n, k, :], out_offset=None, in_=x,
                                        in_offset=bass.IndirectOffsetOnAxis(ap=idx_slot[0:n, k:k + 1], axis=0),
                                        ).then_inc(gathered[k], 16)

            for k in range(BODY):
                gather(0, k, first=True)
            with pool.Fori(1, BODIES) as body:
                t0 = body * BODY
                for k in range(BODY):
                    gather(t0, k)
            for k in range(TILES - BODIES * BODY):
                gather(BODIES * BODY, k, LAST if BODIES * BODY + k == TILES - 1 else P)

            with pool.Fori(0, FULL // 4) as four:
                g0 = four * 4
                for slot in range(4):
                    pool.wait_ge(sig_done, 2 + g0 + slot + 1)
                    pool.wait_ge(x_in[slot], g0 * 4 + 16)
                    pool.tensor_tensor(yout[:, slot, :, :], yout[:, slot, :, :], xin[:, slot, :, :],
                                       ALU.add).then_inc(summed, 1)
            for g in range(FULL - FULL % 4, GROUPS):
                slot = g % 4
                pool.wait_ge(sig_done, 2 + g + (2 if g == FULL else 1))
                pool.wait_ge(x_in[slot], 16 * (g // 4) + 16 + (16 if g == FULL else 0))
                whole = GROUP if g < FULL else (N - g * GROUP * P) // P
                ins = pool.tensor_tensor(yout[:, slot, 0:whole, :], yout[:, slot, 0:whole, :],
                                         xin[:, slot, 0:whole, :], ALU.add)
                if g == FULL:
                    left = N % P
                    ins.then_inc(pool_step, 1)
                    pool.wait_ge(pool_step, 2)
                    ins = pool.tensor_tensor(yout[0:left, slot, whole, :], yout[0:left, slot, whole, :],
                                             xin[0:left, slot, whole, :], ALU.add)
                ins.then_inc(summed, 1)

        @block.scalar
        def _(act):
            def tick(t0, k, edge):
                t = t0 + k
                m = k % BODY
                if not edge or 0 <= t < TILES:
                    act.wait_ge(norm_ready, (t0 // 4) + k // 4 + 1)
                    if not edge or t >= 4:
                        act.wait_ge(turned, t - 4 + 1)
                    n = LAST if edge and t == TILES - 1 else P
                    nc.scalar.activation(u[0:n, k % 4, :], xg[0:n, m, :], ACT.Relu, bias=negmr[0:n, m:m + 1],
                                         scale=rstd[0:n, m:m + 1]).then_inc(ln_done, 1)
                if not edge or 1 <= t <= TILES:
                    b = (k - 1) % 2
                    n = LAST if edge and t == TILES else P
                    act.wait_ge(turned, t)
                    if not edge or t >= 5:
                        act.wait_ge(multiplied, t - 4)
                    nc.scalar.activation(msg_t[:, (k - 1) % 4, :, 0:n],
                                         bank[:, b, 0:D].rearrange("p (c e) -> p c e", c=KD)[:, :, 0:n],
                                         ACT.Relu).then_inc(relu_done, 1)
                if k % 4 == (3 - LEAD + 1) % 4:
                    q = t + LEAD - 4
                    if not edge or 0 <= q < TILES:
                        m4 = (k + LEAD - 4) % BODY
                        n = P
                        act.wait_ge(mv_done, q + 4)
                        nc.scalar.activation(rstd[:, m4:m4 + 4], mv[:, m4:m4 + 4, 1], ACT.Sqrt,
                                             bias=eps[:, 0:1]).then_inc(std_done, 1)

            act.wait_ge(const_set, 6)
            stage1(act, tick)

            act.wait_ge(diff_ready, 1)
            nc.scalar.activation(val[:, 0:H, :], val[:, 0:H, :], ACT.Exp).then_inc(exp_done, 1)
            act.wait_ge(diff_ready, 2)
            nc.scalar.activation(run[:, H:K, :], run[:, H:K, :], ACT.Exp).then_inc(exp_done, 1)

            act.wait_ge(tables_ready, 1)
            act.wait_ge(wgt_ready, 1)
            act.sem_inc(sig_done, 2)
            x_rows = x[0:FULL * GROUP * P, :].rearrange("(t p) d -> p t d", p=P)
            o_rows = out[0:FULL * GROUP * P, :].rearrange("(t p) d -> p t d", p=P)
            last_row = (FULL * GROUP + LAST_WHOLE) * P

            def load_x(g, slot):
                act.dma_start(xin[:, slot, :, :], x_rows[:, bass.ds(g * GROUP, GROUP), :]).then_inc(x_in[slot], 16)

            def load_last_x():
                slot = FULL % XS
                act.dma_start(xin[:, slot, 0:LAST_WHOLE, :],
                              x[FULL * GROUP * P:last_row, :].rearrange("(t p) d -> p t d", p=P)
                              ).then_inc(x_in[slot], 16)
                act.dma_start(xin[0:N % P, slot, LAST_WHOLE, :], x[last_row:N, :]).then_inc(x_in[slot], 16)

            def sigmoid(g, slot):
                extra = act.value_load(extras_by[:, bass.ds(g, 1)], min_val=1, max_val=TP + 1)
                act.wait_ge(stepped, 8 * g + 16)
                act.wait_ge(extra_done, extra)
                b = GROUP * (slot % 2)
                nc.scalar.activation(yout[:, slot, :, :], bank[:, b:b + GROUP, 0:T], ACT.Sigmoid).then_inc(sig_done, 1)

            def store(g, slot):
                act.wait_ge(summed, g + 1)
                act.dma_start(o_rows[:, bass.ds(g * GROUP, GROUP), :], yout[:, slot, :, :]).then_inc(stored[slot], 16)

            for g in range(3):
                load_x(g, g)
            for g in range(4):
                sigmoid(g, g)
                if g:
                    store(g - 1, g - 1)
                load_x(g + 3, (g + 3) % 4)
            with act.Fori(1, LOOPED // 4) as four:
                g0 = four * 4
                for slot in range(4):
                    act.wait_ge(stored[slot], 4 * g0)
                    sigmoid(g0 + slot, slot)
                    store(g0 + slot - 1, (slot - 1) % 4)
                    load_x(g0 + slot + 3, (slot + 3) % 4)
            for g in range(LOOPED, FULL):
                slot = g % 4
                act.wait_ge(stored[slot], 16 * (g // 4))
                sigmoid(g, slot)
                store(g - 1, (g - 1) % 4)
                if g + 3 < FULL:
                    load_x(g + 3, (g + 3) % 4)
                elif g + 3 == FULL:
                    load_last_x()
            slot = FULL % 4
            act.wait_ge(stored[slot], 16 * (FULL // 4))
            act.wait_ge(stepped, 2 * NODES + 8)
            act.wait_ge(extra_done, act.value_load(extras_by[:, FULL:FULL + 1], min_val=1, max_val=TP + 1))
            b = GROUP * (slot % 2)
            nc.scalar.activation(yout[:, slot, 0:LAST_WHOLE, :], bank[:, b:b + LAST_WHOLE, 0:T],
                                 ACT.Sigmoid).then_inc(sig_done, 1)
            nc.scalar.activation(yout[0:N % P, slot, LAST_WHOLE, :], bank[0:N % P, b + LAST_WHOLE, 0:T],
                                 ACT.Sigmoid).then_inc(sig_done, 1)
            store(FULL - 1, (FULL - 1) % 4)
            act.wait_ge(summed, GROUPS)
            act.dma_start(out[FULL * GROUP * P:last_row, :].rearrange("(t p) d -> p t d", p=P),
                          yout[:, slot, 0:LAST_WHOLE, :]).then_inc(stored[slot], 16)
            act.dma_start(out[last_row:N, :], yout[0:N % P, slot, LAST_WHOLE, :]).then_inc(stored[slot], 16)
            for k in range(YS):
                act.wait_ge(stored[k], 16 * len(range(k, GROUPS, YS)) + (16 if k == slot else 0))

        @block.tensor
        def _(pe):
            pe.wait_ge(const_set, 6)
            pe.wait_ge(src_f32, 1)
            for b in range(BLK):
                last = nc.tensor.transpose(bank[:, 6, b * P:(b + 1) * P], src_f[:, b, :], ident[:, :])
            last.then_inc(src_turned, 1)
            pe.wait_ge(w_in, 96)
            for c in range(KD):
                for t in range(KT):
                    last = nc.tensor.transpose(bank[:, 7, c * T + t * P:c * T + (t + 1) * P],
                                               w_nat[:, t, c * P:(c + 1) * P], ident[:, :])
            last.then_inc(w_turned, 1)
            for t in range(KT):
                last = nc.tensor.transpose(bank[:, 5, t * K:(t + 1) * K], qg[:, t * P:(t + 1) * P],
                                           ident[0:K, 0:K])
            last.then_inc(qg_turned, 1)
            pe.wait_ge(q_t_ready, 1)
            pe.wait_ge(b_ready, 1)
            for c in range(KD + 1):
                for t in range(KT):
                    lhs = b_rep[:, t, :] if c == KD else w_nat[:, t, c * P:(c + 1) * P]
                    last = nc.tensor.matmul(bank[:, 4, c * K:(c + 1) * K], lhs, q_t[:, t, :],
                                            start=(t == 0), stop=(t == KT - 1))
            last.then_inc(wq_done, 1)

            def by_node_tile(rows, sel, b0, done_sem):
                for w in range(2):
                    for b in range(BLK):
                        last = nc.tensor.matmul(bank[:, b0 + w, 0:NODES], rows(b), sel[:, w, b, :],
                                                start=(b == 0), stop=(b == BLK - 1))
                for b in range(BLK):
                    last = nc.tensor.transpose(bank[:, b0 + 2, b * P:(b + 1) * P], rows(b), ident[:, :])
                last.then_inc(done_sem, 1)

            pe.wait_ge(before_ready, 1)
            for b in range(BLK):
                nc.tensor.matmul(bank[:, 0, 0:NP1], ones[:, :], before[:, b, :], start=(b == 0), stop=(b == BLK - 1))
            for b in range(BLK):
                last = nc.tensor.matmul(bank[:, 1, b * P:(b + 1) * P], ones[:, :], diag[:, b, :],
                                        start=True, stop=True)
            last.then_inc(lo_summed, 1)
            pe.wait_ge(sel_ready, 1)
            by_node_tile(lambda b: dst_f[:, b, :], sel_0, 2, rel_summed)
            pe.wait_ge(tables_ready, 1)

            def tick(t0, k, edge):
                t = t0 + k
                if not edge or 0 <= t < TILES:
                    n = LAST if edge and t == TILES - 1 else P
                    pe.wait_ge(added, t + 1)
                    if not edge or t >= 2:
                        pe.wait_ge(relu_done, t - 1)
                    for c in range(KD):
                        last = nc.tensor.transpose(bank[:, k % 2, c * P:c * P + n], u[0:n, k % 4, c * P:(c + 1) * P],
                                                   ident[0:n, 0:n])
                    last.then_inc(turned, 1)
                if not edge or 1 <= t <= TILES:
                    n = LAST if edge and t == TILES else P
                    pe.wait_ge(relu_done, t)
                    if not edge or t >= 5:
                        pe.wait_ge(p_out, t - 4)
                    for c in range(KD):
                        last = nc.tensor.matmul(bank[0:n, 2 + (k - 1) % 4, 0:NT], msg_t[:, (k - 1) % 4, c, 0:n],
                                                w_all[:, c, :], start=(c == 0), stop=(c == KD - 1))
                    last.then_inc(multiplied, 1)

            stage1(pe, tick)

            pe.wait_ge(p_out, TILES)
            for k in range(K):
                for b in range(BLK):
                    last = nc.tensor.transpose(bank[:, k // 2, (k % 2) * TP + b * P:(k % 2) * TP + (b + 1) * P],
                                               logits[:, b * P:(b + 1) * P, k], ident[:, :])
            last.then_inc(rows_turned, 1)

            def turn_ends(cols, m, count):
                pe.wait_ge(totals_ready, count)
                for side in range(2):
                    for b in range(BLK):
                        last = nc.tensor.transpose(bank[0:m, 5, side * TP + b * P:side * TP + (b + 1) * P],
                                                   cols(b, side), ident[:, :])
                last.then_inc(ends_turned, 1)

            def turn_carries(m, count):
                pe.wait_ge(carries_ready, count)
                for b in range(BLK):
                    for side in range(2):
                        o = (2 * b + side) * C
                        last = nc.tensor.transpose(bank[:, 4, o:o + m], row_b[0:m, 3 + side, b * P:(b + 1) * P],
                                                   ident[0:m, 0:m])
                last.then_inc(carries_turned, 1)

            edge_of = lambda b, side: b * P + (P - 1) * side
            turn_ends(lambda b, side: ends[:, b, side, :], C, 1)
            turn_ends(lambda b, side: tot[:, 0:H, edge_of(b, side)], H, 2)
            turn_carries(H, 1)
            turn_ends(lambda b, side: tot[:, 0:C, edge_of(b, side)], C, 3)
            turn_carries(C, 2)
            pe.wait_ge(c_ready, 1)
            by_node_tile(lambda b: flag[:, 2, b * P:(b + 1) * P], sel_1, 0, wgt_summed)

            def fixed(j, k, b, slot):
                pe.wait_ge(spread_ready, 2 * j + 2)
                for w in range(2):
                    nc.tensor.matmul(bank[:, b, 0:T], spread[:, 2 * k + w, :], p_keep[:, bass.ds(slot + w, 1), :],
                                     start=(w == 0), stop=True, skip_group_check=True).then_inc(stepped, 1)

            def extras(j, b):
                n_extra = pe.value_load(extras_of[:, bass.ds(j, 1)], min_val=0, max_val=TILES)
                with pe.If(n_extra):
                    i0 = pe.value_load(lo_i[:, bass.ds(j, 1)], min_val=0, max_val=TILES - 1)
                    with pe.Fori(0, n_extra) as n:
                        i = nc.s_assert_within(i0 + n + 2, 0, TILES - 1, skip_runtime_bounds_check_because=in_range)
                        nth = pe.value_load(ordinal[:, bass.ds(i, 1)], min_val=1, max_val=TILES)
                        slot = pe.value_load(slot_of[:, bass.ds(i, 1)], min_val=0, max_val=RING - 1)
                        pe.wait_ge(extra_ready, nth)
                        nc.tensor.matmul(bank[:, b, 0:T], spread_x[:, :], p_keep[:, bass.ds(slot, 1), :],
                                         start=False, stop=True, skip_group_check=True).then_inc(extra_done, 1)

            def group(g, half):
                w0 = pe.value_load(slots_of[:, bass.ds(g, 1)], min_val=0, max_val=(1 << 21) - 1)
                w1 = pe.value_load(flags_of[:, bass.ds(g, 1)], min_val=0, max_val=255)
                slots = [w0 & 127, (w0 >> 7) & 127, w0 >> 14, w1 >> 1]
                pe.wait_ge(sig_done, g + 1)
                with pe.If(w1 & 1):
                    for k in range(GROUP):
                        fixed(GROUP * g + k, k, GROUP * half + k, slots[k])
                        extras(GROUP * g + k, GROUP * half + k)
                with pe.Else():
                    for k in range(GROUP):
                        fixed(GROUP * g + k, k, GROUP * half + k, slots[k])

            pe.wait_ge(wgt_ready, 1)
            pe.sem_inc(stepped, 8)
            pe.sem_inc(extra_done, 1)
            with pe.Fori(0, FULL // 2) as two:
                for half in range(2):
                    group(2 * two + half, half)
            group(FULL - 1, 0)
            w0 = pe.value_load(slots_of[:, FULL:FULL + 1], min_val=0, max_val=(1 << 21) - 1)
            pe.wait_ge(sig_done, FULL + 1)
            for k in range(LAST_WHOLE + 1):
                fixed(GROUP * FULL + k, k, GROUP + k, (w0 >> (7 * k)) & 127)
                extras(GROUP * FULL + k, GROUP + k)

        @block.vector
        def _(dve):
            steps = [0]

            def then(ins):
                steps[0] += 1
                ins.then_inc(dve_step, 1)
                dve.wait_ge(dve_step, steps[0])

            v = nc.vector
            dve.wait_ge(const_set, 6)
            dve.wait_ge(src_in, 48)
            v.tensor_copy(src_f, src_i).then_inc(src_f32, 1)
            v.tensor_copy(count_f[:, :], count_i)
            v.tensor_copy(tile_f[:, :], tile_i[:, :])
            dve.wait_ge(dst_in, 48)
            then(v.tensor_copy(dst_f[:, :, :], dst_i))
            dve.wait_ge(src_turned, 1)
            v.tensor_copy(idx[:, :], bank[:, 6, 0:TP]).then_inc(idx_ready, 1)
            dve.wait_ge(w_in, 96)
            v.tensor_copy(b_rep, b_col.unsqueeze(2).broadcast_to([P, KT, P])).then_inc(b_ready, 1)
            dve.wait_ge(w_turned, 1)
            v.tensor_copy(w_all[:, :, 0:T], bank[:, 7, :].rearrange("p (c t) -> p c t", c=KD))
            dve.wait_ge(qg_turned, 1)
            v.tensor_copy(q_t, bank[:, 5, 0:KT * K].rearrange("p (c k) -> p c k", c=KT)).then_inc(q_t_ready, 1)
            then(v.tensor_scalar(node_of[:, :], dst_f[:, :, P - 1], float(N - 1), None, ALU.min))
            then(v.tensor_copy(node_i[:, :], node_of[:, :]))
            then(v.tensor_scalar(node_i[:, :], node_i[:, :], SHIFT, None, ALU.arith_shift_right))
            then(v.tensor_copy(node_of[:, :], node_i[:, :]))
            for b in range(BLK):
                v.tensor_scalar(before[:, b, :], count_f[:, :], node_of[:, b:b + 1], None, ALU.is_gt)
                ins = v.tensor_scalar(diag[:, b, :], ident[:, :], node_of[:, b:b + 1], None, ALU.mult)
            then(ins)
            dve.sem_inc(before_ready, 1)
            dve.wait_ge(wq_done, 1)
            v.tensor_copy(w_all[:, :, T:NT], bank[:, 4, 0:KD * K].rearrange("p (c k) -> p c k", c=KD))
            v.tensor_copy(bias[:, T:NT], bank[:, 4, KD * K:(KD + 1) * K]).then_inc(w_ready, 1)
            dve.wait_ge(lo_summed, 1)
            node_row = tmp[0][:, 0:TP]
            v.tensor_copy(node_row, bank[:, 1, 0:TP])
            then(v.tensor_scalar(lo[:, :], bank[:, 0, 0:NP1], float(TILES - 1), None, ALU.min))
            for w in range(2):
                for b in range(BLK):
                    ins = v.tensor_scalar(sel_0[:, w, b, :], lo[:, 0:NODES], float(w), tile_f[:, b:b + 1],
                                          ALU.add, ALU.is_equal)
            then(ins)
            dve.sem_inc(sel_ready, 1)
            same_node, nth = tmp[1][:, 0:TP + 1], tmp[2][:, 0:TP]
            then(v.memset(tmp[1], 0.0))
            then(v.tensor_tensor(same_node[:, 1:TP], node_row[:, 1:TP], node_row[:, 0:TP - 1], ALU.is_equal))
            v.memset(nth[:, 0:1], 0.0)
            ones_row = tmp[3][:, 0:NP1]
            then(v.memset(ones_row, 1.0))
            then(v.tensor_tensor_scan(nth[:, 1:TP], ones_row[:, 0:TP - 1], same_node[:, 0:TP - 1], 0.0,
                                      ALU.mult, ALU.add))
            v.tensor_copy(ordinal, nth[96:97])
            v.tensor_scalar(free_extra, nth[32:33], 1.0, None, ALU.add)
            then(v.scalar_tensor_tensor(tmp[4][0:1, 0:TP], node_row[0:1], 2.0, same_node[0:1, 0:TP], ALU.mult, ALU.add))
            v.tensor_scalar(free_fixed, tmp[4][0:1, 0:TP], 1.0 + 8.0, None, ALU.add)

            def slots(to, tiles, t1):
                then(v.tensor_scalar(t1, tiles, float(RING), -float(RING), ALU.is_ge, ALU.mult))
                then(v.tensor_tensor(to, t1, tiles, ALU.add))

            then(v.tensor_copy(tmp[2][64:65, 0:TP], count_f[64:65, 0:TP]))
            slots(tmp[4][64:65, 0:TP], tmp[2][64:65, 0:TP], tmp[1][64:65, 0:TP])
            then(v.tensor_copy(slot_of, tmp[4][64:65, 0:TP]))
            dve.wait_ge(rel_summed, 1)
            for w in range(2):
                v.scalar_tensor_tensor(rel[:, w, :], count_f[:, 0:NODES], -float(P), bank[:, 2 + w, 0:NODES],
                                       ALU.mult, ALU.add)
            v.scalar_tensor_tensor(rel_x[:, 1:TP], node_row[:, 0:TP - 1], -float(P), bank[:, 4, 1:TP],
                                   ALU.mult, ALU.add)
            n_x, x_by, slot = tmp[1], tmp[2], tmp[4]
            then(v.tensor_copy(lo_i, lo[0:1, :]))
            then(v.tensor_scalar(tmp[0][64:65], lo[64:65, :], 2.0, float(TILES), ALU.add, ALU.min))
            then(v.tensor_copy(wants_of, tmp[0][64:65]))
            v.memset(n_x, 0.0)
            then(v.tensor_tensor(x_by[:, 0:NODES], lo[:, 1:NP1], lo[:, 0:NODES], ALU.subtract))
            then(v.tensor_scalar(n_x[:, 0:NODES], x_by[:, 0:NODES], -1.0, 0.0, ALU.add, ALU.max))
            v.tensor_copy(extras_of, n_x[32:33, :])
            then(v.tensor_tensor_scan(x_by, ones_row, n_x, 1.0, ALU.mult, ALU.add))
            v.tensor_copy(extras_by, x_by[0:1, GROUP - 1::GROUP])
            slots(slot, lo[:, :], tmp[0])
            by4 = lambda a, n: a[:, n:n + (GROUPS - 1) * GROUP + 1:GROUP]
            a, b_, flag_g = tmp[0][:, 0:GROUPS], tmp[0][:, GROUPS:2 * GROUPS], tmp[3][:, 0:GROUPS]
            then(v.scalar_tensor_tensor(a, by4(slot, 2), 128.0, by4(slot, 1), ALU.mult, ALU.add))
            then(v.scalar_tensor_tensor(a, a, 128.0, by4(slot, 0), ALU.mult, ALU.add))
            v.tensor_copy(slots_of[:, 0:GROUPS], a[64:65])
            then(v.tensor_tensor(b_, by4(n_x, 0), by4(n_x, 1), ALU.add))
            then(v.tensor_tensor(b_, b_, by4(n_x, 2), ALU.add))
            then(v.tensor_tensor(b_, b_, by4(n_x, 3), ALU.add))
            then(v.tensor_scalar(flag_g, b_, 0.0, None, ALU.is_gt))
            then(v.scalar_tensor_tensor(a, by4(slot, 3), 2.0, flag_g, ALU.mult, ALU.add))
            v.tensor_copy(flags_of[:, 0:GROUPS], a[96:97])
            then(v.tensor_scalar(b_, by4(lo, 3), 1.0, float(TILES - 1), ALU.add, ALU.min))
            then(v.tensor_scalar(b_, b_, 1.0, 2.0, ALU.add, ALU.mult))
            then(v.tensor_tensor(needs_of, b_[32:33], flag_g[32:33], ALU.add))
            dve.sem_inc(tables_ready, 1)

            def tick(t0, k, edge):
                t = t0 + k
                n, m = t + LEAD, (k + LEAD) % BODY
                ahead = not edge or 0 <= n < TILES
                na = LAST if edge and n == TILES - 1 else P
                if ahead:
                    dve.wait_ge(gathered[m], (t0 if not edge else 0) + 16 * ((k + LEAD) // BODY) + 16)
                    v.bn_stats(stats[0:na, m, :], xg[0:na, m, :]).then_inc(stats_done, 1)
                if not edge or 0 <= t < TILES:
                    r = LAST if edge and t == TILES - 1 else P
                    q = (k // 4) % 4
                    dve.wait_ge(ln_done, t + 1)
                    more = 16 if edge and t >= BODIES * BODY else 0
                    dve.wait_ge(ea_in[q], (t0 if not edge else 0) + 16 * (k // BODY) + 16 + more)
                    v.tensor_tensor(u[0:r, k % 4, :], u[0:r, k % 4, :], ea[0:r, k % BODY, :],
                                    ALU.add).then_inc(added, 1)
                if not edge or LAG <= t < TILES + LAG:
                    e = t - LAG
                    b = 2 + (k - LAG) % 4
                    r = LAST if edge and e == TILES - 1 else P
                    late = (e >= RING) if edge else t0_late[0]
                    if late:
                        slot = RING + (k - LAG - RING) % STAGE
                        if not edge or e >= RING + STAGE:
                            w = (2 * t0 - 2 * SPLIT * BODY + 16 * (k // 8)) if not edge else 16 * ((e - RING) // 8)
                            w = w + 16
                            dve.wait_ge(spilled[(slot - RING) // 4], w)
                        to = p_keep[:, slot:slot + 1, :].rearrange("p t d -> p (t d)")
                        if r < P:
                            v.memset(to, 0.0).then_inc(padded, 1)
                            dve.wait_ge(padded, 1)
                    else:
                        to = p_keep[:, bass.ds(e, 1), :].rearrange("p t d -> p (t d)")
                    dve.wait_ge(multiplied, e + 1)
                    v.tensor_tensor(logits[0:r, bass.ds(e, 1), :].rearrange("p t k -> p (t k)"), bank[0:r, b, T:NT],
                                    bias[0:r, T:NT], ALU.add)
                    v.tensor_tensor(to[0:r], bank[0:r, b, 0:T], bias[0:r, 0:T], ALU.add).then_inc(p_out, 1)
                if k % 4 == (3 - LEAD) % 4 and ahead:
                    dve.wait_ge(stats_done, n + 1)
                    dve.sem_inc(stats_seen, 1)
                    for a in range(4):
                        na = LAST if edge and n - 3 + a == TILES - 1 else P
                        v.bn_aggr(mv[0:na, m - 3 + a, :], stats[0:na, m - 3 + a, :]).then_inc(mv_done, 1)
                if k % 4 == 3:
                    q = t + LEAD - 5
                    if not edge or 0 <= q < TILES:
                        m4 = (k + LEAD - 5) % BODY
                        c = (t0 // 4) + (k + LEAD - 5) // 4 + 1
                        dve.wait_ge(std_done, c)
                        v.reciprocal(rstd[:, m4:m4 + 4], rstd[:, m4:m4 + 4]).then_inc(rstd_done, 1)
                        dve.wait_ge(rstd_done, c)
                        v.scalar_tensor_tensor(negmr[:, m4:m4 + 4], mv[:, m4:m4 + 4, 0], -1.0, rstd[:, m4:m4 + 4],
                                               ALU.mult, ALU.mult).then_inc(norm_ready, 1)

            stage1(dve, tick)

            same, same_next, end, in_first, in_last, neg = (flag[:, n, :] for n in range(6))
            per_blk = lambda a: a.rearrange("p (b e) -> p b e", b=BLK)
            dst_rows = dst_f[:, :, :].rearrange("p b e -> p (b e)")
            dve.wait_ge(turned, TILES)
            dve.wait_ge(multiplied, TILES)
            v.memset(same, 0.0)
            then(v.memset(same_next, 0.0))
            v.tensor_tensor(per_blk(same)[:, :, 1:P], dst_f[:, :, 1:P], dst_f[:, :, 0:P - 1], ALU.is_equal)
            then(v.tensor_tensor(per_blk(same_next)[:, :, 0:P - 1], dst_f[:, :, 1:P], dst_f[:, :, 0:P - 1],
                                 ALU.is_equal))
            v.tensor_scalar(end, same_next, -1.0, 1.0, ALU.mult, ALU.add)
            v.tensor_scalar(neg, same, 1.0, BIG, ALU.subtract, ALU.mult)
            for b in range(BLK):
                sl = slice(b * P, (b + 1) * P)
                v.tensor_scalar(in_first[:, sl], dst_f[:, b, :], dst_f[:, b, 0:1], None, ALU.is_equal)
                v.tensor_scalar(in_last[:, sl], dst_f[:, b, :], dst_f[:, b, P - 1:P], None, ALU.is_equal)
                for side in range(2):
                    c = (P - 1) * side
                    ins = v.tensor_copy(ends[:, b, side, :], dst_f[:, b, c:c + 1].broadcast_to([P, C]))
            then(ins)
            dve.sem_inc(totals_ready, 1)
            v.memset(val[:, 2 * H, :], 1.0)
            dve.wait_ge(rows_turned, 1)
            for g in range(K // 2):
                ins = v.tensor_copy(val[:, 2 * g:2 * g + 2, :], bank[:, g, :].rearrange("p (k e) -> p k e", k=2))
            then(ins)
            first_d, last_d, cont, whole_t, fwd_keep, bwd_keep, first_v = (row_a[:, n, :] for n in range(7))
            last_v, keep, give, from_left, from_right, cneg = (row_b[:, n, :] for n in range(6))
            dve.wait_ge(ends_turned, 1)
            v.tensor_copy(first_d[:, 0:TP], bank[0:C, 5, 0:TP])
            v.memset(cont, 0.0)
            v.memset(fwd_keep, 0.0)
            v.memset(bwd_keep, 0.0)
            then(v.tensor_copy(last_d[:, 0:TP], bank[0:C, 5, TP:2 * TP]))
            v.tensor_tensor(cont[:, 1:TP], first_d[:, 1:TP], last_d[:, 0:TP - 1], ALU.is_equal)
            then(v.tensor_tensor(whole_t[:, 0:TP], first_d[:, 0:TP], last_d[:, 0:TP], ALU.is_equal))
            v.tensor_tensor(fwd_keep[:, 1:TP], cont[:, 1:TP], whole_t[:, 0:TP - 1], ALU.mult)
            v.tensor_tensor(bwd_keep[:, 0:TP - 1], cont[:, 1:TP], whole_t[:, 1:TP], ALU.mult)
            then(v.tensor_scalar(cneg, cont, 1.0, BIG, ALU.subtract, ALU.mult))

            def over_edges(k, ops, data0):
                for n in range(k):
                    ins = v.tensor_tensor_scan(run[:, n, :], data0, val[:, n, :], 0.0, *ops)
                then(ins)
                then(v.tensor_tensor(run[:, 0:k, :], run[:, 0:k, :], end.unsqueeze(1).broadcast_to([P, k, RW]),
                                     ALU.mult))
                for n in range(k):
                    ins = v.tensor_tensor_scan(tot[:, n, ::-1], same_next[:, ::-1], run[:, n, ::-1], 0.0,
                                               ALU.mult, ALU.add)
                then(ins)
                dve.sem_inc(totals_ready, 1)

            def over_tiles(k, ops, is_max, count):
                dve.wait_ge(ends_turned, count + 1)
                v.tensor_copy(first_v[0:k, 0:TP], bank[0:k, 5, 0:TP])
                then(v.tensor_copy(last_v[0:k, 0:TP], bank[0:k, 5, TP:2 * TP]))
                for side in range(2):
                    r = slice(0, k)
                    here = slice(1, TP) if side == 0 else slice(0, TP - 1)
                    there = slice(0, TP - 1) if side == 0 else slice(1, TP)
                    keeps = (fwd_keep, bwd_keep)[side]
                    gives = (last_v, first_v)[side]
                    to = (from_left, from_right)[side]
                    then(v.memset(give[r, 0:TP], -BIG if is_max else 0.0))
                    then(v.tensor_tensor(give[r, here], cont[r, 1:TP], gives[r, there], ALU.mult))
                    if is_max:
                        then(v.tensor_tensor(give[r, here], give[r, here], cneg[r, 1:TP], ALU.add))
                        then(v.tensor_scalar(keep[r, 0:TP], keeps[r, 0:TP], 1.0, BIG, ALU.subtract, ALU.mult))
                        d0 = keep[r, 0:TP]
                    else:
                        d0 = keeps[r, 0:TP]
                    back = slice(None, None, -1 if side else 1)
                    then(v.tensor_tensor_scan(to[r, 0:TP][:, back], d0[:, back], give[r, 0:TP][:, back],
                                              -BIG if is_max else 0.0, *ops))
                dve.sem_inc(carries_ready, 1)
                dve.wait_ge(carries_turned, count)
                then(v.tensor_copy(carry[:, :, :, 0:k], bank[:, 4, 0:BLK * 2 * C].rearrange(
                    "p (b s k) -> p b s k", b=BLK, s=2)[:, :, :, 0:k]))
                for side in range(2):
                    mask = (in_first, in_last)[side]
                    if is_max:
                        then(v.tensor_scalar(neg, mask, 1.0, BIG, ALU.subtract, ALU.mult))
                        mask = neg
                    for n in range(k):
                        for b in range(BLK):
                            sl = slice(b * P, (b + 1) * P)
                            ins = v.scalar_tensor_tensor(tot[:, n, sl], mask[:, sl], carry[:, b, side, n:n + 1],
                                                         tot[:, n, sl], ALU.add if is_max else ALU.mult,
                                                         ALU.max if is_max else ALU.add)
                    then(ins)

            over_edges(H, (ALU.add, ALU.max), neg)
            over_tiles(H, (ALU.add, ALU.max), True, 1)
            v.tensor_tensor(val[:, 0:H, :], val[:, 0:H, :], tot[:, 0:H, :], ALU.subtract).then_inc(diff_ready, 1)
            dve.wait_ge(exp_done, 1)
            over_edges(C, (ALU.mult, ALU.add), same)
            over_tiles(C, (ALU.mult, ALU.add), False, 2)
            over_h = lambda a: a.unsqueeze(1).broadcast_to([P, H, RW])
            then(v.tensor_scalar(run[:, 2 * H, :], tot[:, 2 * H, :], 1.0, None, ALU.max))
            then(v.reciprocal(run[:, 2 * H, :], run[:, 2 * H, :]))
            then(v.tensor_tensor(run[:, H:K, :], tot[:, H:K, :], over_h(run[:, 2 * H, :]), ALU.mult))
            for h in range(H):
                ins = v.tensor_scalar(run[:, H + h, :], run[:, H + h, :], bg_b[:, h:h + 1], None, ALU.add)
            then(ins)
            then(v.tensor_tensor(run[:, 0:2, :], run[:, H:H + 2, :], run[:, H + 2:K, :], ALU.max))
            then(v.tensor_tensor(run[:, 0, :], run[:, 0, :], run[:, 1, :], ALU.max))
            v.tensor_tensor(run[:, H:K, :], run[:, H:K, :], over_h(run[:, 0, :]), ALU.subtract).then_inc(diff_ready, 1)
            then(v.tensor_scalar(tot[:, 0:H, :], tot[:, 0:H, :], 1e-9, None, ALU.max))
            then(v.reciprocal(tot[:, 0:H, :], tot[:, 0:H, :]))
            then(v.tensor_tensor(tot[:, 0:H, :], tot[:, 0:H, :], val[:, 0:H, :], ALU.mult))
            dve.wait_ge(exp_done, 2)
            v.tensor_tensor(tot[:, 0:H, :], tot[:, 0:H, :], run[:, H:K, :], ALU.mult)
            then(v.tensor_tensor(run[:, 0:2, :], run[:, H:H + 2, :], run[:, H + 2:K, :], ALU.add))
            then(v.tensor_tensor(run[:, 0, :], run[:, 0, :], run[:, 1, :], ALU.add))
            then(v.reciprocal(run[:, 0, :], run[:, 0, :]))
            then(v.tensor_tensor(tot[:, 0:2, :], tot[:, 0:2, :], tot[:, 2:4, :], ALU.add))
            then(v.tensor_tensor(tot[:, 0, :], tot[:, 0, :], tot[:, 1, :], ALU.add))
            then(v.tensor_tensor(flag[:, 2, :], tot[:, 0, :], run[:, 0, :], ALU.mult))
            for w in range(2):
                for b in range(BLK):
                    ins = v.tensor_scalar(sel_1[:, w, b, :], lo[:, 0:NODES], float(w), tile_f[:, b:b + 1],
                                          ALU.add, ALU.is_equal)
            then(ins)
            dve.sem_inc(c_ready, 1)
            dve.wait_ge(wgt_summed, 1)
            v.tensor_copy(wgt[:, :, :], bank[:, 0:2, 0:NODES])
            then(v.tensor_copy(wgt_x[:, :], bank[:, 2, 0:TP]))
            dve.sem_inc(wgt_ready, 1)

            def spread_fixed(j, k):
                dve.wait_ge(stepped, 2 * j + 2)
                for w in range(2):
                    v.tensor_scalar(spread[:, 2 * k + w, :], count_f[:, 0:P], rel[:, w, bass.ds(j, 1)],
                                    wgt[:, w, bass.ds(j, 1)], ALU.is_equal, ALU.mult).then_inc(spread_ready, 1)

            def spread_extras(j):
                n_extra = dve.value_load(extras_of[:, bass.ds(j, 1)], min_val=0, max_val=TILES)
                with dve.If(n_extra):
                    i0 = dve.value_load(lo_i[:, bass.ds(j, 1)], min_val=0, max_val=TILES - 1)
                    with dve.Fori(0, n_extra) as n:
                        i = nc.s_assert_within(i0 + n + 2, 0, TILES - 1, skip_runtime_bounds_check_because=in_range)
                        nth = dve.value_load(ordinal[:, bass.ds(i, 1)], min_val=1, max_val=TILES)
                        dve.wait_ge(p_ready, i + 1)
                        dve.wait_ge(extra_done, nth)
                        v.tensor_scalar(spread_x[:, :], count_f[:, 0:P], rel_x[:, bass.ds(i, 1)],
                                        wgt_x[:, bass.ds(i, 1)], ALU.is_equal, ALU.mult).then_inc(extra_ready, 1)

            def wait_for_p(j):
                tiles = dve.value_load(wants_of[:, bass.ds(j, 1)], min_val=1, max_val=TILES)
                dve.wait_ge(p_ready, tiles)

            def spread_group(g):
                word = dve.value_load(needs_of[:, bass.ds(g, 1)], min_val=2, max_val=2 * TILES + 1)
                with dve.If(word & 1):
                    for k in range(GROUP):
                        j = GROUP * g + k
                        wait_for_p(j)
                        spread_fixed(j, k)
                        spread_extras(j)
                with dve.Else():
                    dve.wait_ge(p_ready, word >> 1)
                    for k in range(GROUP):
                        spread_fixed(GROUP * g + k, k)

            with dve.Fori(0, FULL) as g:
                spread_group(g)
            for k in range(LAST_WHOLE + 1):
                j = GROUP * FULL + k
                wait_for_p(j)
                spread_fixed(j, k)
                spread_extras(j)


_INS = ['x', 'src', 'dst', 'edge_attr_256', 'L0_gnn_W_fc', 'L0_gnn_b_fc', 'L0_gnn_Q', 'L0_gnn_Wg', 'L0_gnn_bg']
_OUTS = [((50000, 256), 'float32')]


def kernel(**inputs):
    import numpy as _np
    import concourse.bacc as _bacc
    from concourse import mybir as _mybir
    from concourse.bass_utils import run_bass_kernel_spmd as _run

    nc = _bacc.Bacc("TRN2", target_bir_lowering=False, num_devices=1)
    arrays, args = {}, []
    for name in _INS:
        a = _np.ascontiguousarray(inputs[name])
        arrays[f"in_{name}_dram"] = a
        args.append(nc.dram_tensor(f"in_{name}_dram", a.shape, _mybir.dt.from_np(a.dtype), kind="ExternalInput").ap())
    for i, (shape, dtype) in enumerate(_OUTS):
        dt = _mybir.dt.from_np(_np.dtype(dtype))
        args.append(nc.dram_tensor(f"out_{i}_dram", shape, dt, kind="ExternalOutput").ap())
    gnn_layer(nc, *args)
    r = _run(nc, [arrays], core_ids=[0])
    return r.results[0]["out_0_dram"]
```

```python
from contextlib import ExitStack

import concourse.bass as bass
from concourse import mybir

F32 = mybir.dt.float32
I32 = mybir.dt.int32
ALU = mybir.AluOpType
ACT = mybir.ActivationFunctionType
AX = mybir.AxisListType

P = 128
BIG = 1.0e30
LN_EPS = 1e-5
BODY = 16
LEAD = 7
LAG = 4


def gnn_layer(nc, x, src, dst, edge_attr, w_fc, b_fc, q_w, g_w, b_g, out):
    N, D = x.shape
    E = src.shape[0]
    T = w_fc.shape[0]
    H = q_w.shape[0]
    K = 2 * H
    C = 2 * H + 1
    KD, KT = D // P, T // P
    TILES = -(-E // P)
    LAST = E - (TILES - 1) * P
    BLK = -(-TILES // P)
    TP = BLK * P
    NODES = -(-N // P)
    NP1 = NODES + 1
    PAD = 1 << 16
    SHIFT = P.bit_length() - 1
    NT = T + K
    BODIES = TILES // BODY
    SPLIT = 8
    RING = SPLIT * BODY - LAG
    STAGE = 8
    SPILL = TILES - RING
    BEHIND = 8
    assert RING % 4 == 0 and SPILL % 4 == 0 and SPILL <= RING and (RING + LAG) % BODY == 0

    GROUP = 4
    GROUPS = -(-NODES // GROUP)
    FULL = N // (GROUP * P)
    assert GROUPS == FULL + 1 and FULL % 2 == 1
    ROUND = 4
    assert FULL % ROUND == 1
    LAST_WHOLE = (N - FULL * GROUP * P) // P
    LOOPED = (FULL - 3) // 4 * 4
    XS, YS = 4, 4
    assert FULL % 4 == 1 and LAST_WHOLE == 2 and N % P and LOOPED + 3 < FULL

    scratch = nc.dram_tensor("p_spill", [SPILL * P, T], F32).ap()

    with ExitStack() as ctx:
        def sb(name, shape, dt=F32):
            return ctx.enter_context(nc.sbuf_tensor(name, shape, dt))

        def sem(name):
            return ctx.enter_context(nc.semaphore(name))

        bank = ctx.enter_context(nc.psum_tensor("bank", [P, 8, 512], F32))

        p_keep = sb("p_keep", [P, RING + STAGE, T])
        arena = sb("arena", [P, 10240])
        logits = sb("logits", [P, TP, K])
        w_all = sb("w_all", [P, KD, NT])
        bias = sb("bias", [P, NT])
        ident = sb("ident", [P, P])
        ones = sb("ones", [P, P])
        count_f = sb("count_f", [P, NP1])
        lo = sb("lo", [P, NP1])
        rel = sb("rel", [P, 2, NODES])
        wgt = sb("wgt", [P, 2, NODES])
        rel_x = sb("rel_x", [P, TP])
        wgt_x = sb("wgt_x", [P, TP])
        dst_f = sb("dst_f", [P, BLK, P])
        idx = sb("idx", [P, TP], I32)
        idx_slot = sb("idx_slot", [P, BODY], I32)
        spread = sb("spread", [P, 2 * GROUP, P])
        stats = sb("stats", [P, BODY, 6])
        mv = sb("mv", [P, BODY, 2])
        rstd = sb("rstd", [P, BODY])
        negmr = sb("negmr", [P, BODY])
        eps = sb("eps", [P, 1])
        bg_b = sb("bg_b", [P, H])
        tile_f = sb("tile_f", [P, BLK])
        tile_i = sb("tile_i", [P, BLK], I32)
        spread_x = sb("spread_x", [P, 3, P])
        node_of = sb("node_of", [P, BLK])
        node_i = sb("node_i", [P, BLK], I32)
        by_tile = sb("by_tile", [P, TP], I32)
        free_fixed, free_extra = (by_tile[32 * n:32 * n + 1, :] for n in range(2))
        by_node = sb("by_node", [P, NP1], I32)
        extras_of, slots_of = (by_node[32 * n:32 * n + 1, :] for n in range(2))
        more = sb("more", [P, GROUPS], I32)
        extras_by, needs_of = more[0:1, :], more[32:33, :]

        o = 0
        xg = arena[:, o:o + BODY * D].rearrange("p (t d) -> p t d", d=D); o += BODY * D
        ea = arena[:, o:o + BODY * D].rearrange("p (t d) -> p t d", d=D); o += BODY * D
        u = arena[:, o:o + 4 * D].rearrange("p (t d) -> p t d", d=D); o += 4 * D
        msg_t = arena[:, o:o + 4 * D].rearrange("p (t c e) -> p t c e", c=KD, e=P); o += 4 * D
        assert o <= 10240
        o = 0
        RW = BLK * P
        val = arena[:, o:o + C * RW].rearrange("p (k e) -> p k e", k=C); o += C * RW
        run = arena[:, o:o + C * RW].rearrange("p (k e) -> p k e", k=C); o += C * RW
        tot = arena[:, o:o + C * RW].rearrange("p (k e) -> p k e", k=C); o += C * RW
        flag = arena[:, o:o + 6 * RW].rearrange("p (k e) -> p k e", k=6); o += 6 * RW
        row_b = arena[0:C, o:o + 6 * (TP + 1)].rearrange("p (k t) -> p k t", k=6); o += 6 * (TP + 1)
        carry = arena[:, o:o + BLK * 2 * C].rearrange("p (b s k) -> p b s k", b=BLK, s=2); o += BLK * 2 * C
        assert o <= 10240
        row_a = logits[0:C, :, :].rearrange("p t k -> p (t k)")[:, 0:7 * (TP + 1)].rearrange("p (k t) -> p k t", k=7)
        sel_1 = arena[:, C * RW:C * RW + 2 * BLK * NODES].rearrange("p (w b j) -> p w b j", w=2, b=BLK)
        assert 2 * BLK * NODES <= C * RW
        ends = tot[:, 0, 0:BLK * 2 * C].rearrange("p (b s k) -> p b s k", b=BLK, s=2)
        xin = arena[:, 0:XS * GROUP * D].rearrange("p (s q d) -> p s q d", s=XS, q=GROUP)
        yout = arena[:, XS * GROUP * D:(XS + YS) * GROUP * D].rearrange("p (s q d) -> p s q d", s=YS, q=GROUP)
        tail = p_keep[:, RING - 30:RING, :].rearrange("p t d -> p (t d)")
        o = 0
        w_nat = tail[:, o:o + KT * D].rearrange("p (c d) -> p c d", c=KT); o += KT * D
        b_rep = tail[:, o:o + KT * P].rearrange("p (c e) -> p c e", c=KT); o += KT * P
        q_t = tail[:, o:o + KT * K].rearrange("p (c k) -> p c k", c=KT); o += KT * K
        qg = tail[0:K, o:o + T]; o += T
        b_col = tail[:, o:o + KT]; o += KT
        before = tail[:, o:o + BLK * NP1].rearrange("p (b j) -> p b j", b=BLK); o += BLK * NP1
        sel_0 = tail[:, o:o + 2 * BLK * NODES].rearrange("p (w b j) -> p w b j", w=2, b=BLK); o += 2 * BLK * NODES
        diag = tail[:, o:o + TP].rearrange("p (b t) -> p b t", b=BLK); o += TP
        count_i = tail[:, o:o + NP1].bitcast(I32); o += NP1
        tmp = [tail[:, o + n * NP1:o + (n + 1) * NP1] for n in range(5)]; o += 5 * NP1
        src_f = tail[:, o:o + TP].rearrange("p (b e) -> p b e", b=BLK); o += TP
        assert o <= 30 * T
        src_i = p_keep[:, RING - 32, :].rearrange("p (b e) -> p b e", b=BLK).bitcast(I32)
        dst_i = p_keep[:, RING - 31, :].rearrange("p (b e) -> p b e", b=BLK).bitcast(I32)

        pads_set = sem("pads_set")
        src_in, dst_in, w_in = sem("src_in"), sem("dst_in"), sem("w_in")
        const_set = sem("const_set")
        src_f32, src_turned, idx_ready = sem("src_f32"), sem("src_turned"), sem("idx_ready")
        w_turned, qg_turned, q_t_ready, b_ready = sem("w_turned"), sem("qg_turned"), sem("q_t_ready"), sem("b_ready")
        wq_done, w_ready = sem("wq_done"), sem("w_ready")
        before_ready, lo_summed, sel_ready = sem("before_ready"), sem("lo_summed"), sem("sel_ready")
        rel_summed = sem("rel_summed")
        tables_ready = sem("tables_ready")
        dve_step, pool_step = sem("dve_step"), sem("pool_step")
        idx_copied, idx_seen, stats_seen = sem("idx_copied"), sem("idx_seen"), sem("stats_seen")
        gathered = [sem(f"gathered{k}") for k in range(BODY)]
        ea_in = [sem(f"ea_in{k}") for k in range(4)]
        stats_done, mv_done = sem("stats_done"), sem("mv_done")
        std_done, rstd_done, norm_ready = sem("std_done"), sem("rstd_done"), sem("norm_ready")
        ln_done, added, turned, relu_done = sem("ln_done"), sem("added"), sem("turned"), sem("relu_done")
        multiplied, p_out, padded = sem("multiplied"), sem("p_out"), sem("padded")
        spilled = [sem("spilled0"), sem("spilled1")]
        rows_turned, ends_turned, carries_ready = sem("rows_turned"), sem("ends_turned"), sem("carries_ready")
        totals_ready, carries_turned = sem("totals_ready"), sem("carries_turned")
        diff_ready, exp_done = sem("diff_ready"), sem("exp_done")
        c_ready, wgt_summed, wgt_ready = sem("c_ready"), sem("wgt_summed"), sem("wgt_ready")
        spread_ready, stepped = sem("spread_ready"), sem("stepped")
        extra_ready, extra_done = sem("extra_ready"), sem("extra_done")
        p_ready, reloaded = sem("p_ready"), sem("reloaded")
        sig_done, summed = sem("sig_done"), sem("summed")
        x_in = [sem(f"x_in{k}") for k in range(XS)]
        stored = [sem(f"stored{k}") for k in range(YS)]

        t0_late = [False]

        def stage1(eng, tick):
            for k in range(-LEAD, BODY):
                tick(0, k, True)
            for a, b in ((1, SPLIT), (SPLIT, BODIES - 1)):
                t0_late[0] = a == SPLIT
                with eng.Fori(a, b) as body:
                    t0 = body * BODY
                    for k in range(BODY):
                        tick(t0, k, False)
            for k in range((BODIES - 1) * BODY, TILES + LAG):
                tick(0, k, True)

        in_range = "the extras of node tile j are the tiles lo[j] + 2 .. lo[j + 1], and lo is at most TILES - 1"

        assert RING <= 128 and TILES + 128 - RING < 256

        def node_word(eng, j):
            word = eng.value_load(extras_of[:, bass.ds(j, 1)], min_val=0, max_val=(1 << 24) - 1)
            return word >> 16, (word >> 8) & 255, word & 255

        def tile_of(i0, n):
            return nc.s_assert_within(i0 + n + 2, 0, TILES - 1, skip_runtime_bounds_check_because=in_range)

        block = ctx.enter_context(nc.Block())

        @block.sync
        def _(sp):
            sp.wait_ge(pads_set, 2)
            for half in range(2):
                sp.sem_inc(spilled[half], 16)
            for dram, tile, done_ in ((src, src_i, src_in), (dst, dst_i, dst_in)):
                whole = (TILES - 1) * P
                sp.dma_start(tile[:, 0, :], dram[0:P * P].rearrange("(t e) -> t e", e=P)).then_inc(done_, 16)
                sp.dma_start(tile[0:TILES - 1 - P, 1, :],
                             dram[P * P:whole].rearrange("(t e) -> t e", e=P)).then_inc(done_, 16)
                sp.dma_start(tile[TILES - 1 - P:TILES - P, 1, 0:LAST],
                             dram[whole:E].rearrange("(t e) -> t e", t=1)).then_inc(done_, 16)
            sp.dma_start(w_nat, w_fc.rearrange("(c p) d -> p c d", p=P)).then_inc(w_in, 16)
            sp.dma_start(qg[0:H, :], q_w).then_inc(w_in, 16)
            sp.dma_start(qg[H:K, :], g_w).then_inc(w_in, 16)
            with nc.allow_non_contiguous_dma(reason="one column of biases, once"):
                sp.dma_start(b_col, b_fc.rearrange("(c p) -> p c", p=P)).then_inc(w_in, 16)
            sp.dma_start(bias[:, 0:T], b_fc.rearrange("(a n) -> a n", a=1).broadcast_to([P, T])).then_inc(w_in, 16)
            sp.dma_start(bg_b[:, :], b_g.rearrange("(a n) -> a n", a=1).broadcast_to([P, H])).then_inc(w_in, 16)

            ea_rows = edge_attr[0:(TILES - 1) * P, :].rearrange("(t p) d -> p t d", p=P)

            def load_ea(t0, quad, first=False):
                if not first:
                    sp.wait_ge(added, t0 + 4 * quad - BODY + 4)
                sp.dma_start(ea[:, 4 * (quad % 4):4 * (quad % 4) + 4, :],
                             ea_rows[:, bass.ds(t0 + 4 * quad, 4), :]).then_inc(ea_in[quad % 4], 16)

            for quad in range(4):
                load_ea(0, quad, True)
            with sp.Fori(1, SPLIT) as body:
                t0 = body * BODY
                for quad in range(4):
                    load_ea(t0, quad)

            def spill(n4, half):
                sp.wait_ge(p_out, RING + n4 + 4)
                sp.dma_start(scratch[bass.ds(n4 * P, 4 * P), :].rearrange("(t p) d -> p t d", p=P),
                             p_keep[:, RING + 4 * half:RING + 4 * half + 4, :]).then_inc(spilled[half], 16)

            for quad in range(4):
                load_ea(SPLIT * BODY, quad)
                if 4 * quad >= BEHIND:
                    spill(4 * quad - BEHIND, quad % 2)
            with sp.Fori(SPLIT + 1, BODIES) as body:
                t0 = body * BODY
                for quad in range(4):
                    load_ea(t0, quad)
                    spill(t0 + 4 * quad - SPLIT * BODY - BEHIND, quad % 2)
            t0 = BODIES * BODY
            sp.wait_ge(added, t0 - BODY + 4)
            sp.dma_start(ea[:, 0:3, :], ea_rows[:, t0:t0 + 3, :]).then_inc(ea_in[0], 16)
            sp.dma_start(ea[0:LAST, 3, :], edge_attr[(TILES - 1) * P:E, :]).then_inc(ea_in[0], 16)
            n4 = t0 - SPLIT * BODY - BEHIND
            while n4 < SPILL:
                spill(n4, (n4 // 4) % 2)
                n4 += 4
            for half in range(2):
                sp.wait_ge(spilled[half], 16 + 16 * len(range(half, SPILL // 4, 2)))

            sp.wait_ge(tables_ready, 1)
            sp.wait_ge(c_ready, 1)
            sp.sem_inc(p_ready, RING)

            def reload(n, slots):
                fixed_steps = sp.value_load(free_fixed[:, bass.ds(n, 1)], min_val=1, max_val=2 * NODES + 8)
                extra_steps = sp.value_load(free_extra[:, bass.ds(n, 1)], min_val=1, max_val=TP + 2)
                sp.wait_ge(stepped, fixed_steps)
                sp.wait_ge(extra_done, extra_steps)
                for slot in slots:
                    sp.dma_start(p_keep[:, bass.ds(slot, 1), :].rearrange("p t d -> p (t d)"),
                                 scratch[bass.ds(n * P, P), :]).then_inc(reloaded, 16)

            reload(0, (0, RING))
            sp.wait_ge(reloaded, 32)
            sp.sem_inc(p_ready, 1)
            with sp.Fori(1, SPILL) as n:
                reload(n, (n,))
                sp.wait_ge(reloaded, 16 * n + 32)
                sp.sem_inc(p_ready, 1)
            sp.sem_inc(p_ready, 1)

        @block.gpsimd
        def _(pool):
            pool.memset(src_i, 0).then_inc(pads_set, 1)
            pool.memset(dst_i, PAD).then_inc(pads_set, 1)
            pool.memset(ident[:, :], 0.0).then_inc(pool_step, 1)
            pool.wait_ge(pool_step, 1)
            pool.affine_select(out=ident[:, :], in_=ident[:, :], compare_op=ALU.not_equal, fill=1.0, base=0,
                               pattern=[[-1, P]], channel_multiplier=1).then_inc(const_set, 1)
            pool.memset(ones[:, :], 1.0).then_inc(const_set, 1)
            pool.iota(count_i, pattern=[[1, NP1]], base=0, channel_multiplier=0).then_inc(const_set, 1)
            pool.iota(tile_i[:, :], pattern=[[P, BLK]], base=0, channel_multiplier=1).then_inc(const_set, 1)
            pool.memset(eps[:, :], LN_EPS).then_inc(const_set, 1)
            pool.memset(logits[:, TILES - 1:TP, :], 0.0).then_inc(const_set, 1)
            pool.wait_ge(idx_ready, 1)

            def gather(t0, k, n=P, first=False):
                if k % 4 == 0:
                    if not first:
                        pool.wait_ge(ln_done, t0 + k - BODY + 4)
                    pool.tensor_copy(idx_slot[:, k:k + 4], idx[:, bass.ds(t0 + k, 4)]).then_inc(idx_copied, 1)
                    pool.wait_ge(idx_copied, (t0 // 4) + k // 4 + 1)
                    pool.sem_inc(idx_seen, 1)
                pool.indirect_dma_start(out=xg[0:n, k, :], out_offset=None, in_=x,
                                        in_offset=bass.IndirectOffsetOnAxis(ap=idx_slot[0:n, k:k + 1], axis=0),
                                        ).then_inc(gathered[k], 16)

            for k in range(BODY):
                gather(0, k, first=True)
            with pool.Fori(1, BODIES) as body:
                t0 = body * BODY
                for k in range(BODY):
                    gather(t0, k)
            for k in range(TILES - BODIES * BODY):
                gather(BODIES * BODY, k, LAST if BODIES * BODY + k == TILES - 1 else P)

            with pool.Fori(0, FULL // 4) as four:
                g0 = four * 4
                for slot in range(4):
                    pool.wait_ge(sig_done, 2 + g0 + slot + 1)
                    pool.wait_ge(x_in[slot], g0 * 4 + 16)
                    pool.tensor_tensor(yout[:, slot, :, :], yout[:, slot, :, :], xin[:, slot, :, :],
                                       ALU.add).then_inc(summed, 1)
            for g in range(FULL - FULL % 4, GROUPS):
                slot = g % 4
                pool.wait_ge(sig_done, 2 + g + (2 if g == FULL else 1))
                pool.wait_ge(x_in[slot], 16 * (g // 4) + 16 + (16 if g == FULL else 0))
                whole = GROUP if g < FULL else (N - g * GROUP * P) // P
                ins = pool.tensor_tensor(yout[:, slot, 0:whole, :], yout[:, slot, 0:whole, :],
                                         xin[:, slot, 0:whole, :], ALU.add)
                if g == FULL:
                    left = N % P
                    ins.then_inc(pool_step, 1)
                    pool.wait_ge(pool_step, 2)
                    ins = pool.tensor_tensor(yout[0:left, slot, whole, :], yout[0:left, slot, whole, :],
                                             xin[0:left, slot, whole, :], ALU.add)
                ins.then_inc(summed, 1)

        @block.scalar
        def _(act):
            def tick(t0, k, edge):
                t = t0 + k
                m = k % BODY
                if not edge or 0 <= t < TILES:
                    act.wait_ge(norm_ready, (t0 // 4) + k // 4 + 1)
                    if not edge or t >= 4:
                        act.wait_ge(turned, t - 4 + 1)
                    n = LAST if edge and t == TILES - 1 else P
                    nc.scalar.activation(u[0:n, k % 4, :], xg[0:n, m, :], ACT.Relu, bias=negmr[0:n, m:m + 1],
                                         scale=rstd[0:n, m:m + 1]).then_inc(ln_done, 1)
                if not edge or 1 <= t <= TILES:
                    b = (k - 1) % 2
                    n = LAST if edge and t == TILES else P
                    act.wait_ge(turned, t)
                    if not edge or t >= 5:
                        act.wait_ge(multiplied, t - 4)
                    nc.scalar.activation(msg_t[:, (k - 1) % 4, :, 0:n],
                                         bank[:, b, 0:D].rearrange("p (c e) -> p c e", c=KD)[:, :, 0:n],
                                         ACT.Relu).then_inc(relu_done, 1)
                if k % 4 == (3 - LEAD + 1) % 4:
                    q = t + LEAD - 4
                    if not edge or 0 <= q < TILES:
                        m4 = (k + LEAD - 4) % BODY
                        n = P
                        act.wait_ge(mv_done, q + 4)
                        nc.scalar.activation(rstd[:, m4:m4 + 4], mv[:, m4:m4 + 4, 1], ACT.Sqrt,
                                             bias=eps[:, 0:1]).then_inc(std_done, 1)

            act.wait_ge(const_set, 6)
            stage1(act, tick)

            act.wait_ge(diff_ready, 1)
            nc.scalar.activation(val[:, 0:H, :], val[:, 0:H, :], ACT.Exp).then_inc(exp_done, 1)
            act.wait_ge(diff_ready, 2)
            nc.scalar.activation(run[:, H:K, :], run[:, H:K, :], ACT.Exp).then_inc(exp_done, 1)

            act.wait_ge(tables_ready, 1)
            act.wait_ge(wgt_ready, 1)
            act.sem_inc(sig_done, 2)
            x_rows = x[0:FULL * GROUP * P, :].rearrange("(t p) d -> p t d", p=P)
            o_rows = out[0:FULL * GROUP * P, :].rearrange("(t p) d -> p t d", p=P)
            last_row = (FULL * GROUP + LAST_WHOLE) * P

            def load_x(g, slot):
                act.dma_start(xin[:, slot, :, :], x_rows[:, bass.ds(g * GROUP, GROUP), :]).then_inc(x_in[slot], 16)

            def load_last_x():
                slot = FULL % XS
                act.dma_start(xin[:, slot, 0:LAST_WHOLE, :],
                              x[FULL * GROUP * P:last_row, :].rearrange("(t p) d -> p t d", p=P)
                              ).then_inc(x_in[slot], 16)
                act.dma_start(xin[0:N % P, slot, LAST_WHOLE, :], x[last_row:N, :]).then_inc(x_in[slot], 16)

            def sigmoid(g, slot):
                extra = act.value_load(extras_by[:, bass.ds(g, 1)], min_val=1, max_val=TP + 2)
                act.wait_ge(stepped, 8 * g + 16)
                act.wait_ge(extra_done, extra)
                b = GROUP * (slot % 2)
                nc.scalar.activation(yout[:, slot, :, :], bank[:, b:b + GROUP, 0:T], ACT.Sigmoid).then_inc(sig_done, 1)

            def store(g, slot):
                act.wait_ge(summed, g + 1)
                act.dma_start(o_rows[:, bass.ds(g * GROUP, GROUP), :], yout[:, slot, :, :]).then_inc(stored[slot], 16)

            for g in range(3):
                load_x(g, g)
            for g in range(4):
                sigmoid(g, g)
                if g:
                    store(g - 1, g - 1)
                load_x(g + 3, (g + 3) % 4)
            with act.Fori(1, LOOPED // 4) as four:
                g0 = four * 4
                for slot in range(4):
                    act.wait_ge(stored[slot], 4 * g0)
                    sigmoid(g0 + slot, slot)
                    store(g0 + slot - 1, (slot - 1) % 4)
                    load_x(g0 + slot + 3, (slot + 3) % 4)
            for g in range(LOOPED, FULL):
                slot = g % 4
                act.wait_ge(stored[slot], 16 * (g // 4))
                sigmoid(g, slot)
                store(g - 1, (g - 1) % 4)
                if g + 3 < FULL:
                    load_x(g + 3, (g + 3) % 4)
                elif g + 3 == FULL:
                    load_last_x()
            slot = FULL % 4
            act.wait_ge(stored[slot], 16 * (FULL // 4))
            act.wait_ge(stepped, 2 * NODES + 8)
            act.wait_ge(extra_done, act.value_load(extras_by[:, FULL:FULL + 1], min_val=1, max_val=TP + 2))
            b = GROUP * (slot % 2)
            nc.scalar.activation(yout[:, slot, 0:LAST_WHOLE, :], bank[:, b:b + LAST_WHOLE, 0:T],
                                 ACT.Sigmoid).then_inc(sig_done, 1)
            nc.scalar.activation(yout[0:N % P, slot, LAST_WHOLE, :], bank[0:N % P, b + LAST_WHOLE, 0:T],
                                 ACT.Sigmoid).then_inc(sig_done, 1)
            store(FULL - 1, (FULL - 1) % 4)
            act.wait_ge(summed, GROUPS)
            act.dma_start(out[FULL * GROUP * P:last_row, :].rearrange("(t p) d -> p t d", p=P),
                          yout[:, slot, 0:LAST_WHOLE, :]).then_inc(stored[slot], 16)
            act.dma_start(out[last_row:N, :], yout[0:N % P, slot, LAST_WHOLE, :]).then_inc(stored[slot], 16)
            for k in range(YS):
                act.wait_ge(stored[k], 16 * len(range(k, GROUPS, YS)) + (16 if k == slot else 0))

        @block.tensor
        def _(pe):
            pe.wait_ge(const_set, 6)
            pe.wait_ge(src_f32, 1)
            for b in range(BLK):
                last = nc.tensor.transpose(bank[:, 6, b * P:(b + 1) * P], src_f[:, b, :], ident[:, :])
            last.then_inc(src_turned, 1)
            pe.wait_ge(w_in, 96)
            for c in range(KD):
                for t in range(KT):
                    last = nc.tensor.transpose(bank[:, 7, c * T + t * P:c * T + (t + 1) * P],
                                               w_nat[:, t, c * P:(c + 1) * P], ident[:, :])
            last.then_inc(w_turned, 1)
            for t in range(KT):
                last = nc.tensor.transpose(bank[:, 5, t * K:(t + 1) * K], qg[:, t * P:(t + 1) * P],
                                           ident[0:K, 0:K])
            last.then_inc(qg_turned, 1)
            pe.wait_ge(q_t_ready, 1)
            pe.wait_ge(b_ready, 1)
            for c in range(KD + 1):
                for t in range(KT):
                    lhs = b_rep[:, t, :] if c == KD else w_nat[:, t, c * P:(c + 1) * P]
                    last = nc.tensor.matmul(bank[:, 4, c * K:(c + 1) * K], lhs, q_t[:, t, :],
                                            start=(t == 0), stop=(t == KT - 1))
            last.then_inc(wq_done, 1)

            def by_node_tile(rows, sel, b0, done_sem):
                for w in range(2):
                    for b in range(BLK):
                        last = nc.tensor.matmul(bank[:, b0 + w, 0:NODES], rows(b), sel[:, w, b, :],
                                                start=(b == 0), stop=(b == BLK - 1))
                for b in range(BLK):
                    last = nc.tensor.transpose(bank[:, b0 + 2, b * P:(b + 1) * P], rows(b), ident[:, :])
                last.then_inc(done_sem, 1)

            pe.wait_ge(before_ready, 1)
            for b in range(BLK):
                nc.tensor.matmul(bank[:, 0, 0:NP1], ones[:, :], before[:, b, :], start=(b == 0), stop=(b == BLK - 1))
            for b in range(BLK):
                last = nc.tensor.matmul(bank[:, 1, b * P:(b + 1) * P], ones[:, :], diag[:, b, :],
                                        start=True, stop=True)
            last.then_inc(lo_summed, 1)
            pe.wait_ge(sel_ready, 1)
            by_node_tile(lambda b: dst_f[:, b, :], sel_0, 2, rel_summed)
            pe.wait_ge(tables_ready, 1)

            def tick(t0, k, edge):
                t = t0 + k
                if not edge or 0 <= t < TILES:
                    n = LAST if edge and t == TILES - 1 else P
                    pe.wait_ge(added, t + 1)
                    if not edge or t >= 2:
                        pe.wait_ge(relu_done, t - 1)
                    for c in range(KD):
                        last = nc.tensor.transpose(bank[:, k % 2, c * P:c * P + n], u[0:n, k % 4, c * P:(c + 1) * P],
                                                   ident[0:n, 0:n])
                    last.then_inc(turned, 1)
                if not edge or 1 <= t <= TILES:
                    n = LAST if edge and t == TILES else P
                    pe.wait_ge(relu_done, t)
                    if not edge or t >= 5:
                        pe.wait_ge(p_out, t - 4)
                    for c in range(KD):
                        last = nc.tensor.matmul(bank[0:n, 2 + (k - 1) % 4, 0:NT], msg_t[:, (k - 1) % 4, c, 0:n],
                                                w_all[:, c, :], start=(c == 0), stop=(c == KD - 1))
                    last.then_inc(multiplied, 1)

            stage1(pe, tick)

            pe.wait_ge(p_out, TILES)
            for k in range(K):
                for b in range(BLK):
                    last = nc.tensor.transpose(bank[:, k // 2, (k % 2) * TP + b * P:(k % 2) * TP + (b + 1) * P],
                                               logits[:, b * P:(b + 1) * P, k], ident[:, :])
            last.then_inc(rows_turned, 1)

            def turn_ends(cols, m, count):
                pe.wait_ge(totals_ready, count)
                for side in range(2):
                    for b in range(BLK):
                        last = nc.tensor.transpose(bank[0:m, 5, side * TP + b * P:side * TP + (b + 1) * P],
                                                   cols(b, side), ident[:, :])
                last.then_inc(ends_turned, 1)

            def turn_carries(m, count):
                pe.wait_ge(carries_ready, count)
                for b in range(BLK):
                    for side in range(2):
                        o = (2 * b + side) * C
                        last = nc.tensor.transpose(bank[:, 4, o:o + m], row_b[0:m, 3 + side, b * P:(b + 1) * P],
                                                   ident[0:m, 0:m])
                last.then_inc(carries_turned, 1)

            edge_of = lambda b, side: b * P + (P - 1) * side
            turn_ends(lambda b, side: ends[:, b, side, :], C, 1)
            turn_ends(lambda b, side: tot[:, 0:H, edge_of(b, side)], H, 2)
            turn_carries(H, 1)
            turn_ends(lambda b, side: tot[:, 0:C, edge_of(b, side)], C, 3)
            turn_carries(C, 2)
            pe.wait_ge(c_ready, 1)
            by_node_tile(lambda b: flag[:, 2, b * P:(b + 1) * P], sel_1, 0, wgt_summed)

            def fixed(j, k, b, slot):
                pe.wait_ge(spread_ready, 2 * j + 2)
                for w in range(2):
                    nc.tensor.matmul(bank[:, b, 0:T], spread[:, 2 * k + w, :], p_keep[:, bass.ds(slot + w, 1), :],
                                     start=(w == 0), stop=True, skip_group_check=True).then_inc(stepped, 1)

            def node(j, k, b, slot):
                i0, first, n_extra = node_word(pe, j)
                fixed(j, k, b, slot)

                def extra(n, buf):
                    i = tile_of(i0, n)
                    slot = nc.s_assert_within(i - ((i + 128 - RING) >> 7) * RING, 0, RING - 1,
                                              skip_runtime_bounds_check_because=in_range)
                    pe.wait_ge(extra_ready, first + n + 1)
                    nc.tensor.matmul(bank[:, b, 0:T], spread_x[:, buf, :], p_keep[:, bass.ds(slot, 1), :],
                                     start=False, stop=True, skip_group_check=True).then_inc(extra_done, 1)

                with pe.If(n_extra >> 1):
                    with pe.Fori(0, n_extra >> 1) as pair:
                        for h in range(2):
                            extra(2 * pair + h, h)
                with pe.If(n_extra & 1):
                    extra(n_extra - 1, 2)

            def load_word(g):
                return pe.value_load(slots_of[:, bass.ds(g, 1)], min_val=0, max_val=(1 << 29) - 1)

            def slot_in(word, k):
                return (word >> (7 * k)) & 127

            def groups(g0, n):
                word = load_word(g0)
                with pe.If(word >> 28):
                    for i in range(n):
                        g, b = g0 + i, GROUP * (i % 2)
                        w = word if i == 0 else load_word(g)
                        pe.wait_ge(sig_done, g + 1)
                        for k in range(GROUP):
                            node(GROUP * g + k, k, b + k, slot_in(w, k))
                with pe.Else():
                    for i in range(n):
                        g, b = g0 + i, GROUP * (i % 2)
                        w = word if i == 0 else load_word(g)
                        pe.wait_ge(sig_done, g + 1)
                        for k in range(GROUP):
                            fixed(GROUP * g + k, k, b + k, slot_in(w, k))

            pe.wait_ge(wgt_ready, 1)
            pe.sem_inc(stepped, 8)
            pe.sem_inc(extra_done, 2)
            with pe.Fori(0, FULL // ROUND) as r:
                groups(ROUND * r, ROUND)
            groups(FULL - 1, 1)
            w = load_word(FULL)
            pe.wait_ge(sig_done, FULL + 1)
            for k in range(LAST_WHOLE + 1):
                node(GROUP * FULL + k, k, GROUP + k, slot_in(w, k))

        @block.vector
        def _(dve):
            steps = [0]

            def then(ins):
                steps[0] += 1
                ins.then_inc(dve_step, 1)
                dve.wait_ge(dve_step, steps[0])

            v = nc.vector
            dve.wait_ge(const_set, 6)
            dve.wait_ge(src_in, 48)
            v.tensor_copy(src_f, src_i).then_inc(src_f32, 1)
            v.tensor_copy(count_f[:, :], count_i)
            v.tensor_copy(tile_f[:, :], tile_i[:, :])
            dve.wait_ge(dst_in, 48)
            then(v.tensor_copy(dst_f[:, :, :], dst_i))
            dve.wait_ge(src_turned, 1)
            v.tensor_copy(idx[:, :], bank[:, 6, 0:TP]).then_inc(idx_ready, 1)
            dve.wait_ge(w_in, 96)
            v.tensor_copy(b_rep, b_col.unsqueeze(2).broadcast_to([P, KT, P])).then_inc(b_ready, 1)
            dve.wait_ge(w_turned, 1)
            v.tensor_copy(w_all[:, :, 0:T], bank[:, 7, :].rearrange("p (c t) -> p c t", c=KD))
            dve.wait_ge(qg_turned, 1)
            v.tensor_copy(q_t, bank[:, 5, 0:KT * K].rearrange("p (c k) -> p c k", c=KT)).then_inc(q_t_ready, 1)
            then(v.tensor_scalar(node_of[:, :], dst_f[:, :, P - 1], float(N - 1), None, ALU.min))
            then(v.tensor_copy(node_i[:, :], node_of[:, :]))
            then(v.tensor_scalar(node_i[:, :], node_i[:, :], SHIFT, None, ALU.arith_shift_right))
            then(v.tensor_copy(node_of[:, :], node_i[:, :]))
            for b in range(BLK):
                v.tensor_scalar(before[:, b, :], count_f[:, :], node_of[:, b:b + 1], None, ALU.is_gt)
                ins = v.tensor_scalar(diag[:, b, :], ident[:, :], node_of[:, b:b + 1], None, ALU.mult)
            then(ins)
            dve.sem_inc(before_ready, 1)
            dve.wait_ge(wq_done, 1)
            v.tensor_copy(w_all[:, :, T:NT], bank[:, 4, 0:KD * K].rearrange("p (c k) -> p c k", c=KD))
            v.tensor_copy(bias[:, T:NT], bank[:, 4, KD * K:(KD + 1) * K]).then_inc(w_ready, 1)
            dve.wait_ge(lo_summed, 1)
            node_row = tmp[0][:, 0:TP]
            v.tensor_copy(node_row, bank[:, 1, 0:TP])
            then(v.tensor_scalar(lo[:, :], bank[:, 0, 0:NP1], float(TILES - 1), None, ALU.min))
            for w in range(2):
                for b in range(BLK):
                    ins = v.tensor_scalar(sel_0[:, w, b, :], lo[:, 0:NODES], float(w), tile_f[:, b:b + 1],
                                          ALU.add, ALU.is_equal)
            then(ins)
            dve.sem_inc(sel_ready, 1)
            same_node, nth = tmp[1][:, 0:TP + 1], tmp[2][:, 0:TP]
            then(v.memset(tmp[1], 0.0))
            then(v.tensor_tensor(same_node[:, 1:TP], node_row[:, 1:TP], node_row[:, 0:TP - 1], ALU.is_equal))
            v.memset(nth[:, 0:1], 0.0)
            ones_row = tmp[3][:, 0:NP1]
            then(v.memset(ones_row, 1.0))
            then(v.tensor_tensor_scan(nth[:, 1:TP], ones_row[:, 0:TP - 1], same_node[:, 0:TP - 1], 0.0,
                                      ALU.mult, ALU.add))
            v.tensor_scalar(free_extra, nth[32:33], 2.0, None, ALU.add)
            then(v.scalar_tensor_tensor(tmp[4][0:1, 0:TP], node_row[0:1], 2.0, same_node[0:1, 0:TP], ALU.mult, ALU.add))
            v.tensor_scalar(free_fixed, tmp[4][0:1, 0:TP], 1.0 + 8.0, None, ALU.add)

            def slots(to, tiles, t1):
                then(v.tensor_scalar(t1, tiles, float(RING), -float(RING), ALU.is_ge, ALU.mult))
                then(v.tensor_tensor(to, t1, tiles, ALU.add))

            dve.wait_ge(rel_summed, 1)
            for w in range(2):
                v.scalar_tensor_tensor(rel[:, w, :], count_f[:, 0:NODES], -float(P), bank[:, 2 + w, 0:NODES],
                                       ALU.mult, ALU.add)
            v.scalar_tensor_tensor(rel_x[:, 1:TP], node_row[:, 0:TP - 1], -float(P), bank[:, 4, 1:TP],
                                   ALU.mult, ALU.add)
            n_x, x_by, slot, word = tmp[1], tmp[2], tmp[4], tmp[0]
            assert TILES < 256
            v.memset(n_x, 0.0)
            then(v.tensor_tensor(x_by[:, 0:NODES], lo[:, 1:NP1], lo[:, 0:NODES], ALU.subtract))
            then(v.tensor_scalar(n_x[:, 0:NODES], x_by[:, 0:NODES], -1.0, 0.0, ALU.add, ALU.max))
            then(v.tensor_tensor_scan(x_by, ones_row, n_x, 2.0, ALU.mult, ALU.add))
            then(v.scalar_tensor_tensor(word, x_by, -2.0, n_x, ALU.add, ALU.subtract))
            then(v.scalar_tensor_tensor(word, lo[:, :], 256.0, word, ALU.mult, ALU.add))
            then(v.scalar_tensor_tensor(word, word, 256.0, n_x, ALU.mult, ALU.add))
            then(v.tensor_copy(extras_of, word[0:1]))
            v.tensor_copy(extras_by, x_by[0:1, GROUP - 1::GROUP])
            slots(slot, lo[:, :], tmp[0])
            by4 = lambda a, n: a[:, n:n + (GROUPS - 1) * GROUP + 1:GROUP]
            a, b_, flag_g = tmp[0][:, 0:GROUPS], tmp[0][:, GROUPS:2 * GROUPS], tmp[3][:, 0:GROUPS]
            high, flag_r = tmp[0][:, 2 * GROUPS:3 * GROUPS], tmp[3][:, GROUPS:2 * GROUPS]
            then(v.scalar_tensor_tensor(a, by4(slot, 2), 128.0, by4(slot, 1), ALU.mult, ALU.add))
            then(v.scalar_tensor_tensor(a, a, 128.0, by4(slot, 0), ALU.mult, ALU.add))
            low_i, high_i = (src_f[:, n, 0:GROUPS].bitcast(I32) for n in range(2))
            v.tensor_copy(low_i, a)
            then(v.tensor_tensor(b_, by4(n_x, 0), by4(n_x, 1), ALU.add))
            then(v.tensor_tensor(b_, b_, by4(n_x, 2), ALU.add))
            then(v.tensor_tensor(b_, b_, by4(n_x, 3), ALU.add))
            then(v.tensor_scalar(flag_g, b_, 0.0, None, ALU.is_gt))
            then(v.tensor_copy(flag_r, flag_g))
            for n in range(1, ROUND):
                then(v.tensor_tensor(flag_r[:, 0:GROUPS - n], flag_r[:, 0:GROUPS - n], flag_g[:, n:GROUPS], ALU.max))
            then(v.scalar_tensor_tensor(high, flag_r, 128.0, by4(slot, 3), ALU.mult, ALU.add))
            then(v.tensor_scalar(high, high, float(1 << 21), None, ALU.mult))
            then(v.tensor_copy(high_i, high))
            then(v.tensor_tensor(slots_of[:, 0:GROUPS], low_i[32:33], high_i[32:33], ALU.bitwise_or))
            then(v.tensor_scalar(b_, by4(lo, 3), 1.0, float(TILES - 1), ALU.add, ALU.min))
            then(v.tensor_scalar(b_, b_, 1.0, 2.0, ALU.add, ALU.mult))
            then(v.tensor_tensor(needs_of, b_[32:33], flag_g[32:33], ALU.add))
            dve.sem_inc(tables_ready, 1)

            def tick(t0, k, edge):
                t = t0 + k
                n, m = t + LEAD, (k + LEAD) % BODY
                ahead = not edge or 0 <= n < TILES
                na = LAST if edge and n == TILES - 1 else P
                if ahead:
                    dve.wait_ge(gathered[m], (t0 if not edge else 0) + 16 * ((k + LEAD) // BODY) + 16)
                    v.bn_stats(stats[0:na, m, :], xg[0:na, m, :]).then_inc(stats_done, 1)
                if not edge or 0 <= t < TILES:
                    r = LAST if edge and t == TILES - 1 else P
                    q = (k // 4) % 4
                    dve.wait_ge(ln_done, t + 1)
                    more = 16 if edge and t >= BODIES * BODY else 0
                    dve.wait_ge(ea_in[q], (t0 if not edge else 0) + 16 * (k // BODY) + 16 + more)
                    v.tensor_tensor(u[0:r, k % 4, :], u[0:r, k % 4, :], ea[0:r, k % BODY, :],
                                    ALU.add).then_inc(added, 1)
                if not edge or LAG <= t < TILES + LAG:
                    e = t - LAG
                    b = 2 + (k - LAG) % 4
                    r = LAST if edge and e == TILES - 1 else P
                    late = (e >= RING) if edge else t0_late[0]
                    if late:
                        slot = RING + (k - LAG - RING) % STAGE
                        if not edge or e >= RING + STAGE:
                            w = (2 * t0 - 2 * SPLIT * BODY + 16 * (k // 8)) if not edge else 16 * ((e - RING) // 8)
                            w = w + 16
                            dve.wait_ge(spilled[(slot - RING) // 4], w)
                        to = p_keep[:, slot:slot + 1, :].rearrange("p t d -> p (t d)")
                        if r < P:
                            v.memset(to, 0.0).then_inc(padded, 1)
                            dve.wait_ge(padded, 1)
                    else:
                        to = p_keep[:, bass.ds(e, 1), :].rearrange("p t d -> p (t d)")
                    dve.wait_ge(multiplied, e + 1)
                    v.tensor_tensor(logits[0:r, bass.ds(e, 1), :].rearrange("p t k -> p (t k)"), bank[0:r, b, T:NT],
                                    bias[0:r, T:NT], ALU.add)
                    v.tensor_tensor(to[0:r], bank[0:r, b, 0:T], bias[0:r, 0:T], ALU.add).then_inc(p_out, 1)
                if k % 4 == (3 - LEAD) % 4 and ahead:
                    dve.wait_ge(stats_done, n + 1)
                    dve.sem_inc(stats_seen, 1)
                    for a in range(4):
                        na = LAST if edge and n - 3 + a == TILES - 1 else P
                        v.bn_aggr(mv[0:na, m - 3 + a, :], stats[0:na, m - 3 + a, :]).then_inc(mv_done, 1)
                if k % 4 == (5 - LEAD) % 4:
                    q = t + LEAD - 5
                    if not edge or 0 <= q < TILES:
                        m4 = (k + LEAD - 5) % BODY
                        c = (t0 // 4) + (k + LEAD - 5) // 4 + 1
                        dve.wait_ge(std_done, c)
                        v.reciprocal(rstd[:, m4:m4 + 4], rstd[:, m4:m4 + 4]).then_inc(rstd_done, 1)
                        dve.wait_ge(rstd_done, c)
                        v.scalar_tensor_tensor(negmr[:, m4:m4 + 4], mv[:, m4:m4 + 4, 0], -1.0, rstd[:, m4:m4 + 4],
                                               ALU.mult, ALU.mult).then_inc(norm_ready, 1)

            stage1(dve, tick)

            same, same_next, end, in_first, in_last, neg = (flag[:, n, :] for n in range(6))
            per_blk = lambda a: a.rearrange("p (b e) -> p b e", b=BLK)
            dst_rows = dst_f[:, :, :].rearrange("p b e -> p (b e)")
            dve.wait_ge(turned, TILES)
            dve.wait_ge(multiplied, TILES)
            v.memset(same, 0.0)
            then(v.memset(same_next, 0.0))
            v.tensor_tensor(per_blk(same)[:, :, 1:P], dst_f[:, :, 1:P], dst_f[:, :, 0:P - 1], ALU.is_equal)
            then(v.tensor_tensor(per_blk(same_next)[:, :, 0:P - 1], dst_f[:, :, 1:P], dst_f[:, :, 0:P - 1],
                                 ALU.is_equal))
            v.tensor_scalar(end, same_next, -1.0, 1.0, ALU.mult, ALU.add)
            v.tensor_scalar(neg, same, 1.0, BIG, ALU.subtract, ALU.mult)
            for b in range(BLK):
                sl = slice(b * P, (b + 1) * P)
                v.tensor_scalar(in_first[:, sl], dst_f[:, b, :], dst_f[:, b, 0:1], None, ALU.is_equal)
                v.tensor_scalar(in_last[:, sl], dst_f[:, b, :], dst_f[:, b, P - 1:P], None, ALU.is_equal)
                for side in range(2):
                    c = (P - 1) * side
                    ins = v.tensor_copy(ends[:, b, side, :], dst_f[:, b, c:c + 1].broadcast_to([P, C]))
            then(ins)
            dve.sem_inc(totals_ready, 1)
            v.memset(val[:, 2 * H, :], 1.0)
            dve.wait_ge(rows_turned, 1)
            for g in range(K // 2):
                ins = v.tensor_copy(val[:, 2 * g:2 * g + 2, :], bank[:, g, :].rearrange("p (k e) -> p k e", k=2))
            then(ins)
            first_d, last_d, cont, whole_t, fwd_keep, bwd_keep, first_v = (row_a[:, n, :] for n in range(7))
            last_v, keep, give, from_left, from_right, cneg = (row_b[:, n, :] for n in range(6))
            dve.wait_ge(ends_turned, 1)
            v.tensor_copy(first_d[:, 0:TP], bank[0:C, 5, 0:TP])
            v.memset(cont, 0.0)
            v.memset(fwd_keep, 0.0)
            v.memset(bwd_keep, 0.0)
            then(v.tensor_copy(last_d[:, 0:TP], bank[0:C, 5, TP:2 * TP]))
            v.tensor_tensor(cont[:, 1:TP], first_d[:, 1:TP], last_d[:, 0:TP - 1], ALU.is_equal)
            then(v.tensor_tensor(whole_t[:, 0:TP], first_d[:, 0:TP], last_d[:, 0:TP], ALU.is_equal))
            v.tensor_tensor(fwd_keep[:, 1:TP], cont[:, 1:TP], whole_t[:, 0:TP - 1], ALU.mult)
            v.tensor_tensor(bwd_keep[:, 0:TP - 1], cont[:, 1:TP], whole_t[:, 1:TP], ALU.mult)
            then(v.tensor_scalar(cneg, cont, 1.0, BIG, ALU.subtract, ALU.mult))

            def over_edges(k, ops, data0):
                for n in range(k):
                    ins = v.tensor_tensor_scan(run[:, n, :], data0, val[:, n, :], 0.0, *ops)
                then(ins)
                then(v.tensor_tensor(run[:, 0:k, :], run[:, 0:k, :], end.unsqueeze(1).broadcast_to([P, k, RW]),
                                     ALU.mult))
                for n in range(k):
                    ins = v.tensor_tensor_scan(tot[:, n, ::-1], same_next[:, ::-1], run[:, n, ::-1], 0.0,
                                               ALU.mult, ALU.add)
                then(ins)
                dve.sem_inc(totals_ready, 1)

            def over_tiles(k, ops, is_max, count):
                dve.wait_ge(ends_turned, count + 1)
                v.tensor_copy(first_v[0:k, 0:TP], bank[0:k, 5, 0:TP])
                then(v.tensor_copy(last_v[0:k, 0:TP], bank[0:k, 5, TP:2 * TP]))
                for side in range(2):
                    r = slice(0, k)
                    here = slice(1, TP) if side == 0 else slice(0, TP - 1)
                    there = slice(0, TP - 1) if side == 0 else slice(1, TP)
                    keeps = (fwd_keep, bwd_keep)[side]
                    gives = (last_v, first_v)[side]
                    to = (from_left, from_right)[side]
                    then(v.memset(give[r, 0:TP], -BIG if is_max else 0.0))
                    then(v.tensor_tensor(give[r, here], cont[r, 1:TP], gives[r, there], ALU.mult))
                    if is_max:
                        then(v.tensor_tensor(give[r, here], give[r, here], cneg[r, 1:TP], ALU.add))
                        then(v.tensor_scalar(keep[r, 0:TP], keeps[r, 0:TP], 1.0, BIG, ALU.subtract, ALU.mult))
                        d0 = keep[r, 0:TP]
                    else:
                        d0 = keeps[r, 0:TP]
                    back = slice(None, None, -1 if side else 1)
                    then(v.tensor_tensor_scan(to[r, 0:TP][:, back], d0[:, back], give[r, 0:TP][:, back],
                                              -BIG if is_max else 0.0, *ops))
                dve.sem_inc(carries_ready, 1)
                dve.wait_ge(carries_turned, count)
                then(v.tensor_copy(carry[:, :, :, 0:k], bank[:, 4, 0:BLK * 2 * C].rearrange(
                    "p (b s k) -> p b s k", b=BLK, s=2)[:, :, :, 0:k]))
                for side in range(2):
                    mask = (in_first, in_last)[side]
                    if is_max:
                        then(v.tensor_scalar(neg, mask, 1.0, BIG, ALU.subtract, ALU.mult))
                        mask = neg
                    for n in range(k):
                        for b in range(BLK):
                            sl = slice(b * P, (b + 1) * P)
                            ins = v.scalar_tensor_tensor(tot[:, n, sl], mask[:, sl], carry[:, b, side, n:n + 1],
                                                         tot[:, n, sl], ALU.add if is_max else ALU.mult,
                                                         ALU.max if is_max else ALU.add)
                    then(ins)

            over_edges(H, (ALU.add, ALU.max), neg)
            over_tiles(H, (ALU.add, ALU.max), True, 1)
            v.tensor_tensor(val[:, 0:H, :], val[:, 0:H, :], tot[:, 0:H, :], ALU.subtract).then_inc(diff_ready, 1)
            dve.wait_ge(exp_done, 1)
            over_edges(C, (ALU.mult, ALU.add), same)
            over_tiles(C, (ALU.mult, ALU.add), False, 2)
            over_h = lambda a: a.unsqueeze(1).broadcast_to([P, H, RW])
            then(v.tensor_scalar(run[:, 2 * H, :], tot[:, 2 * H, :], 1.0, None, ALU.max))
            then(v.reciprocal(run[:, 2 * H, :], run[:, 2 * H, :]))
            then(v.tensor_tensor(run[:, H:K, :], tot[:, H:K, :], over_h(run[:, 2 * H, :]), ALU.mult))
            for h in range(H):
                ins = v.tensor_scalar(run[:, H + h, :], run[:, H + h, :], bg_b[:, h:h + 1], None, ALU.add)
            then(ins)
            then(v.tensor_tensor(run[:, 0:2, :], run[:, H:H + 2, :], run[:, H + 2:K, :], ALU.max))
            then(v.tensor_tensor(run[:, 0, :], run[:, 0, :], run[:, 1, :], ALU.max))
            v.tensor_tensor(run[:, H:K, :], run[:, H:K, :], over_h(run[:, 0, :]), ALU.subtract).then_inc(diff_ready, 1)
            then(v.tensor_scalar(tot[:, 0:H, :], tot[:, 0:H, :], 1e-9, None, ALU.max))
            then(v.reciprocal(tot[:, 0:H, :], tot[:, 0:H, :]))
            then(v.tensor_tensor(tot[:, 0:H, :], tot[:, 0:H, :], val[:, 0:H, :], ALU.mult))
            dve.wait_ge(exp_done, 2)
            v.tensor_tensor(tot[:, 0:H, :], tot[:, 0:H, :], run[:, H:K, :], ALU.mult)
            then(v.tensor_tensor(run[:, 0:2, :], run[:, H:H + 2, :], run[:, H + 2:K, :], ALU.add))
            then(v.tensor_tensor(run[:, 0, :], run[:, 0, :], run[:, 1, :], ALU.add))
            then(v.reciprocal(run[:, 0, :], run[:, 0, :]))
            then(v.tensor_tensor(tot[:, 0:2, :], tot[:, 0:2, :], tot[:, 2:4, :], ALU.add))
            then(v.tensor_tensor(tot[:, 0, :], tot[:, 0, :], tot[:, 1, :], ALU.add))
            then(v.tensor_tensor(flag[:, 2, :], tot[:, 0, :], run[:, 0, :], ALU.mult))
            for w in range(2):
                for b in range(BLK):
                    ins = v.tensor_scalar(sel_1[:, w, b, :], lo[:, 0:NODES], float(w), tile_f[:, b:b + 1],
                                          ALU.add, ALU.is_equal)
            then(ins)
            dve.sem_inc(c_ready, 1)
            dve.wait_ge(wgt_summed, 1)
            v.tensor_copy(wgt[:, :, :], bank[:, 0:2, 0:NODES])
            then(v.tensor_copy(wgt_x[:, :], bank[:, 2, 0:TP]))
            dve.sem_inc(wgt_ready, 1)

            def spread_fixed(j, k):
                dve.wait_ge(stepped, 2 * j + 2)
                for w in range(2):
                    v.tensor_scalar(spread[:, 2 * k + w, :], count_f[:, 0:P], rel[:, w, bass.ds(j, 1)],
                                    wgt[:, w, bass.ds(j, 1)], ALU.is_equal, ALU.mult).then_inc(spread_ready, 1)

            def spread_node(j, k):
                i0, first, n_extra = node_word(dve, j)
                dve.wait_ge(p_ready, i0 + 2)
                spread_fixed(j, k)

                def extra(n, buf, wait):
                    dve.wait_ge(p_ready, i0 + n + 3)
                    dve.wait_ge(extra_done, first + n + wait)
                    i = tile_of(i0, n)
                    v.tensor_scalar(spread_x[:, buf, :], count_f[:, 0:P], rel_x[:, bass.ds(i, 1)],
                                    wgt_x[:, bass.ds(i, 1)], ALU.is_equal, ALU.mult).then_inc(extra_ready, 1)

                with dve.If(n_extra >> 1):
                    with dve.Fori(0, n_extra >> 1) as pair:
                        for h in range(2):
                            extra(2 * pair + h, h, 1)
                with dve.If(n_extra & 1):
                    extra(n_extra - 1, 2, 2)

            def spread_group(g):
                word = dve.value_load(needs_of[:, bass.ds(g, 1)], min_val=2, max_val=2 * TILES + 1)
                with dve.If(word & 1):
                    for k in range(GROUP):
                        spread_node(GROUP * g + k, k)
                with dve.Else():
                    dve.wait_ge(p_ready, word >> 1)
                    for k in range(GROUP):
                        spread_fixed(GROUP * g + k, k)

            with dve.Fori(0, FULL) as g:
                spread_group(g)
            for k in range(LAST_WHOLE + 1):
                spread_node(GROUP * FULL + k, k)


_INS = ['x', 'src', 'dst', 'edge_attr_256', 'L0_gnn_W_fc', 'L0_gnn_b_fc', 'L0_gnn_Q', 'L0_gnn_Wg', 'L0_gnn_bg']
_OUTS = [((50000, 256), 'float32')]


def kernel(**inputs):
    import numpy as _np
    import concourse.bacc as _bacc
    from concourse import mybir as _mybir
    from concourse.bass_utils import run_bass_kernel_spmd as _run

    nc = _bacc.Bacc("TRN2", target_bir_lowering=False, num_devices=1)
    arrays, args = {}, []
    for name in _INS:
        a = _np.ascontiguousarray(inputs[name])
        arrays[f"in_{name}_dram"] = a
        args.append(nc.dram_tensor(f"in_{name}_dram", a.shape, _mybir.dt.from_np(a.dtype), kind="ExternalInput").ap())
    for i, (shape, dtype) in enumerate(_OUTS):
        dt = _mybir.dt.from_np(_np.dtype(dtype))
        args.append(nc.dram_tensor(f"out_{i}_dram", shape, dt, kind="ExternalOutput").ap())
    gnn_layer(nc, *args)
    r = _run(nc, [arrays], core_ids=[0])
    return r.results[0]["out_0_dram"]
```
